# Optimizing a Trainium2 kernel written in Bass

```python
import numpy as np
import jax
import jax.numpy as jnp

def _softmax(x, axis=-1):
    return jax.nn.softmax(x, axis=axis)

def _gelu(x):
    return jax.nn.gelu(x, approximate=True)

def _silu(x):
    return jax.nn.silu(x)

def _sigmoid(x):
    return jax.nn.sigmoid(x)

def _layernorm(x, axis=-1, eps=1e-05):
    m = jnp.mean(x, axis=axis, keepdims=True)
    v = jnp.var(x, axis=axis, keepdims=True)
    return (x - m) / jnp.sqrt(v + eps)

def _scatter_add(tgt, idx, src, axis=0):
    return tgt.at[idx].add(src)

def _segment_sum(src, seg, n):
    return jax.ops.segment_sum(src, seg, n)
kernel_name = 'mk_xattn_ffn_d2_seqx_r8_99079a'

def setup_inputs(seed: int=0):
    np.random.seed(seed)
    _w = jnp.asarray

    def _rec_inputs():
        import jax
        import jax.numpy as jnp
        _rk = jax.random.key(seed)
        x = -0.0002928 + 1 * jax.random.normal(jax.random.fold_in(_rk, 1), (16, 64, 128), jnp.float32)
        _lenS = 64 - jax.random.randint(jax.random.fold_in(_rk, 7), (16,), 0, max(1, 64 // 4) + 1, jnp.int32)
        _lenS2 = 64 - jax.random.randint(jax.random.fold_in(_rk, 8), (16,), 0, max(1, 64 // 4) + 1, jnp.int32)
        _ctx_1024P = jax.random.normal(jax.random.fold_in(_rk, 11), (16, 16, 128), jnp.float32)
        _ctx_1024c = jax.random.dirichlet(jax.random.fold_in(_rk, 511), 0.3 * jnp.ones((16,), jnp.float32), (16, 64))
        _ctx_1024t = jnp.einsum('bsk,bkd->bsd', _ctx_1024c, _ctx_1024P)
        _ctx_1024t = _ctx_1024t * jax.lax.rsqrt(jnp.mean(jnp.square(_ctx_1024t)) + 1e-12) * 0.953939
        ctx_1024 = -1.39393e-06 + 0.999914 * (_ctx_1024t + 0.3 * jax.random.normal(jax.random.fold_in(_rk, 611), (16, 64, 128), jnp.float32))
        fside_Bx1xSxS2_0 = -4.48278e-06 + 1.00019 * jax.random.normal(jax.random.fold_in(_rk, 13), (16, 1, 64, 64), jnp.float32)
        _validS = jnp.arange(64)[None, :] < _lenS[:, None]
        _validS2 = jnp.arange(64)[None, :] < _lenS2[:, None]
        _causal = jnp.tril(jnp.ones((64, 64), dtype=bool))
        mask_Bx1xSxS2_bf0 = jnp.logical_not(jnp.ones((16, 1, 64, 64), dtype=bool))
        return (x, ctx_1024, fside_Bx1xSxS2_0, mask_Bx1xSxS2_bf0)
    x, ctx_1024, fside_Bx1xSxS2_0, mask_Bx1xSxS2_bf0 = _rec_inputs()

    def _L0_xattn_setup():
        import jax, jax.numpy as jnp
        import numpy as np
        NHEADS = 16
        LN_EPS = 1e-05

        def _layernorm(x, g, b):
            mu = jnp.mean(x, axis=-1, keepdims=True)
            var = jnp.mean(jnp.square(x - mu), axis=-1, keepdims=True)
            return (x - mu) * jax.lax.rsqrt(var + LN_EPS) * g + b
        key = jax.random.key(seed)
        ks = jax.random.split(key, 12)
        B, S, D, F = (2, 256, 128, 512)
        s = 1.0 / np.sqrt(D)
        return {'q': jax.random.normal(ks[0], (B, S, D), jnp.float32), 'k': jax.random.normal(ks[1], (B, S, D), jnp.float32), 'v': jax.random.normal(ks[2], (B, S, D), jnp.float32), 'mask': jnp.zeros((B, 1, S, S), jnp.bool_), 'Wq': jax.random.normal(ks[3], (D, D), jnp.float32) * s, 'Wo': jax.random.normal(ks[4], (D, D), jnp.float32) * s, 'W1': jax.random.normal(ks[5], (F, D), jnp.float32) * s, 'b1': jnp.zeros((F,), jnp.float32), 'W2': jax.random.normal(ks[6], (D, F), jnp.float32) * (1.0 / np.sqrt(F)), 'b2': jnp.zeros((D,), jnp.float32), 'g1': jnp.ones((D,), jnp.float32), 'be1': jnp.zeros((D,), jnp.float32), 'g2': jnp.ones((D,), jnp.float32), 'be2': jnp.zeros((D,), jnp.float32)}
    _L0_xattn_all = _L0_xattn_setup()
    _L0_xattn_in = {k: v for k, v in _L0_xattn_all.items() if k in ('Wq', 'Wo', 'W1', 'b1', 'W2', 'b2', 'g1', 'be1', 'g2', 'be2')}
    del _L0_xattn_all

    def _L0_ffn_setup():
        import jax, jax.numpy as jnp
        import numpy as np
        NEG_INF = -1e+30
        K = 2
        key = jax.random.key(seed)
        ks = jax.random.split(key, 5)
        B, S, D, O, E = (8, 256, 128, 128, 8)
        scale = 1.0 / np.sqrt(D)
        return {'x': jax.random.normal(ks[0], (B, S, D), dtype=jnp.float32), 'gate_w': jax.random.normal(ks[1], (E, D), dtype=jnp.float32) * scale, 'gate_b': jnp.zeros((E,), dtype=jnp.float32), 'expert_w': jax.random.normal(ks[2], (E, O, D), dtype=jnp.float32) * scale, 'expert_b': jnp.zeros((E, O), dtype=jnp.float32)}
    _L0_ffn_all = _L0_ffn_setup()
    _L0_ffn_in = {k: v for k, v in _L0_ffn_all.items() if k in ('gate_w', 'gate_b', 'expert_w', 'expert_b')}
    del _L0_ffn_all

    def _L1_xattn_setup():
        import jax, jax.numpy as jnp
        import numpy as np
        B, S, D_FF = (2, 256, 128)
        NUM_HEADS, D_KV = (16, 64)
        INNER = NUM_HEADS * D_KV
        key = jax.random.key(seed)
        ks = jax.random.split(key, 8)
        scale = 1.0 / np.sqrt(D_FF)
        return {'q': jax.random.normal(ks[0], (B, S, D_FF), jnp.float32), 'k': jax.random.normal(ks[1], (B, S, D_FF), jnp.float32), 'v': jax.random.normal(ks[2], (B, S, D_FF), jnp.float32), 'attn_mask': jax.random.normal(ks[3], (B, 1, S, S), jnp.float32), 'Wq': jax.random.normal(ks[4], (INNER, D_FF), jnp.float32) * scale, 'Wk': jax.random.normal(ks[5], (INNER, D_FF), jnp.float32) * scale, 'Wv': jax.random.normal(ks[6], (INNER, D_FF), jnp.float32) * scale, 'Wo': jax.random.normal(ks[7], (D_FF, INNER), jnp.float32) * scale, 'num_heads': NUM_HEADS}
    _L1_xattn_all = _L1_xattn_setup()
    _L1_xattn_in = {k: v for k, v in _L1_xattn_all.items() if k in ('Wq', 'Wk', 'Wv', 'Wo')}
    del _L1_xattn_all

    def _L1_ffn_setup():
        import jax, jax.numpy as jnp
        import numpy as np
        NUM_EXPERTS = 8
        HIDDEN = 128
        D_FF = 512
        SCALE = 0.8
        SPARSITY = 0.1

        def _perturb_attractive(w, scale=SCALE, sparsity=SPARSITY):
            a = jnp.abs(w)
            flat = a.ravel()
            n = flat.shape[0]
            k = max(1, int(n * sparsity / 2))
            s = jnp.sort(flat)
            thr_bot = s[k - 1]
            thr_top = s[n - k]
            tier = jnp.where(a >= thr_top, -1.0, jnp.where(a <= thr_bot, 1.0, 0.0))
            return w + scale * w * tier

        def _stack_expert_params(w):
            pw = _perturb_attractive(w)
            return jnp.concatenate([w[None], jnp.broadcast_to(pw, (NUM_EXPERTS - 1,) + w.shape)], axis=0)
        key = jax.random.key(seed)
        ks = jax.random.split(key, 6)
        B, S, H, F, E = (2, 256, HIDDEN, D_FF, NUM_EXPERTS)
        return {'x': jax.random.normal(ks[0], (B, S, H), dtype=jnp.float32), 'W1': jax.random.normal(ks[1], (H, F), dtype=jnp.float32) * (1.0 / np.sqrt(H)), 'b1': jax.random.normal(ks[2], (F,), dtype=jnp.float32) * 0.02, 'W2': jax.random.normal(ks[3], (F, H), dtype=jnp.float32) * (1.0 / np.sqrt(F)), 'b2': jax.random.normal(ks[4], (H,), dtype=jnp.float32) * 0.02, 'ln_gamma': jnp.ones((H,), dtype=jnp.float32), 'ln_beta': jnp.zeros((H,), dtype=jnp.float32), 'Wr': jax.random.normal(ks[5], (H, E), dtype=jnp.float32) * (1.0 / np.sqrt(H)), 'br': jnp.zeros((E,), dtype=jnp.float32)}
    _L1_ffn_all = _L1_ffn_setup()
    _L1_ffn_in = {k: v for k, v in _L1_ffn_all.items() if k in ('W1', 'b1', 'W2', 'b2', 'ln_gamma', 'ln_beta', 'Wr', 'br')}
    del _L1_ffn_all
    return {'x': x, 'ctx_1024': ctx_1024, 'fside_Bx1xSxS2_0': fside_Bx1xSxS2_0, 'mask_Bx1xSxS2_bf0': mask_Bx1xSxS2_bf0, 'L0_xattn_Wq': _L0_xattn_in['Wq'], 'L0_xattn_Wo': _L0_xattn_in['Wo'], 'L0_xattn_W1': _L0_xattn_in['W1'], 'L0_xattn_b1': _L0_xattn_in['b1'], 'L0_xattn_W2': _L0_xattn_in['W2'], 'L0_xattn_b2': _L0_xattn_in['b2'], 'L0_xattn_g1': _L0_xattn_in['g1'], 'L0_xattn_be1': _L0_xattn_in['be1'], 'L0_xattn_g2': _L0_xattn_in['g2'], 'L0_xattn_be2': _L0_xattn_in['be2'], 'L0_ffn_gate_w': _L0_ffn_in['gate_w'], 'L0_ffn_gate_b': _L0_ffn_in['gate_b'], 'L0_ffn_expert_w': _L0_ffn_in['expert_w'], 'L0_ffn_expert_b': _L0_ffn_in['expert_b'], 'L1_xattn_Wq': _L1_xattn_in['Wq'], 'L1_xattn_Wk': _L1_xattn_in['Wk'], 'L1_xattn_Wv': _L1_xattn_in['Wv'], 'L1_xattn_Wo': _L1_xattn_in['Wo'], 'L1_ffn_W1': _L1_ffn_in['W1'], 'L1_ffn_b1': _L1_ffn_in['b1'], 'L1_ffn_W2': _L1_ffn_in['W2'], 'L1_ffn_b2': _L1_ffn_in['b2'], 'L1_ffn_ln_gamma': _L1_ffn_in['ln_gamma'], 'L1_ffn_ln_beta': _L1_ffn_in['ln_beta'], 'L1_ffn_Wr': _L1_ffn_in['Wr'], 'L1_ffn_br': _L1_ffn_in['br']}

def reference(x, ctx_1024, fside_Bx1xSxS2_0, mask_Bx1xSxS2_bf0, L0_xattn_Wq, L0_xattn_Wo, L0_xattn_W1, L0_xattn_b1, L0_xattn_W2, L0_xattn_b2, L0_xattn_g1, L0_xattn_be1, L0_xattn_g2, L0_xattn_be2, L0_ffn_gate_w, L0_ffn_gate_b, L0_ffn_expert_w, L0_ffn_expert_b, L1_xattn_Wq, L1_xattn_Wk, L1_xattn_Wv, L1_xattn_Wo, L1_ffn_W1, L1_ffn_b1, L1_ffn_W2, L1_ffn_b2, L1_ffn_ln_gamma, L1_ffn_ln_beta, L1_ffn_Wr, L1_ffn_br):
    import jax
    import jax.numpy as jnp

    def _L0_xattn_ref(q, k, v, mask, Wq, Wo, W1, b1, W2, b2, g1, be1, g2, be2):
        import jax, jax.numpy as jnp
        import numpy as np
        NHEADS = 16
        LN_EPS = 1e-05

        def _layernorm(x, g, b):
            mu = jnp.mean(x, axis=-1, keepdims=True)
            var = jnp.mean(jnp.square(x - mu), axis=-1, keepdims=True)
            return (x - mu) * jax.lax.rsqrt(var + LN_EPS) * g + b
        B, S, D = q.shape
        H, dk = (NHEADS, D // NHEADS)
        qh = (q @ Wq.T).reshape(B, S, H, dk)
        kh = (k @ Wq.T).reshape(B, S, H, dk)
        vh = (v @ Wq.T).reshape(B, S, H, dk)
        score = jnp.einsum('bqhd,bkhd->bhqk', qh, kh) / D ** 0.5
        score = jnp.where(mask, -jnp.inf, score)
        att = jax.nn.softmax(score, axis=-1)
        ctx = jnp.einsum('bhqk,bkhd->bqhd', att, vh).reshape(B, S, D)
        att_out = ctx @ Wo.T
        x = _layernorm(att_out + q, g1, be1)
        h = jax.nn.gelu(x @ W1.T + b1, approximate=False)
        ff = h @ W2.T + b2
        return _layernorm(ff + x, g2, be2)

    def _L0_ffn_ref(x, gate_w, gate_b, expert_w, expert_b):
        import jax, jax.numpy as jnp
        import numpy as np
        NEG_INF = -1e+30
        K = 2
        pooled = x.mean(axis=1)
        logits = pooled @ gate_w.T + gate_b
        topk_vals, _ = jax.lax.top_k(logits, K)
        min_topk = topk_vals[:, -1:]
        masked = jnp.where(logits < min_topk, -jnp.inf, logits)
        gates = jax.nn.softmax(masked, axis=-1)
        expert_out = jax.nn.gelu(jnp.einsum('bsd,eod->beso', x, expert_w) + expert_b[None, :, None, :], approximate=False)
        return jnp.einsum('be,beso->bso', gates, expert_out)

    def _L1_xattn_ref(q, k, v, attn_mask, Wq, Wk, Wv, Wo, num_heads):
        import jax, jax.numpy as jnp
        import numpy as np
        B, S, D_FF = (2, 256, 128)
        NUM_HEADS, D_KV = (16, 64)
        INNER = NUM_HEADS * D_KV
        b, s, _ = q.shape

        def proj_heads(x, W):
            y = jnp.einsum('bsd,ed->bse', x, W)
            return y.reshape(b, s, num_heads, -1).transpose(0, 2, 1, 3)
        qh = proj_heads(q, Wq)
        kh = proj_heads(k, Wk)
        vh = proj_heads(v, Wv)
        scores = jnp.einsum('bhqd,bhkd->bhqk', qh, kh) + attn_mask
        probs = jax.nn.softmax(scores, axis=-1)
        ctx = jnp.einsum('bhqk,bhkd->bhqd', probs, vh)
        ctx = ctx.transpose(0, 2, 1, 3).reshape(b, s, -1)
        return jnp.einsum('bse,de->bsd', ctx, Wo)

    def _L1_ffn_ref(x, W1, b1, W2, b2, ln_gamma, ln_beta, Wr, br):
        import jax, jax.numpy as jnp
        import numpy as np
        NUM_EXPERTS = 8
        HIDDEN = 128
        D_FF = 512
        SCALE = 0.8
        SPARSITY = 0.1

        def _perturb_attractive(w, scale=SCALE, sparsity=SPARSITY):
            a = jnp.abs(w)
            flat = a.ravel()
            n = flat.shape[0]
            k = max(1, int(n * sparsity / 2))
            s = jnp.sort(flat)
            thr_bot = s[k - 1]
            thr_top = s[n - k]
            tier = jnp.where(a >= thr_top, -1.0, jnp.where(a <= thr_bot, 1.0, 0.0))
            return w + scale * w * tier

        def _stack_expert_params(w):
            pw = _perturb_attractive(w)
            return jnp.concatenate([w[None], jnp.broadcast_to(pw, (NUM_EXPERTS - 1,) + w.shape)], axis=0)
        mu = jnp.mean(x, axis=-1, keepdims=True)
        var = jnp.mean(jnp.square(x - mu), axis=-1, keepdims=True)
        h = (x - mu) * jax.lax.rsqrt(var + 1e-05) * ln_gamma + ln_beta
        logits = jnp.einsum('bsh,he->bse', h, Wr) + br
        probs = jax.nn.softmax(logits, axis=-1)
        W1s = _stack_expert_params(W1)
        b1s = _stack_expert_params(b1)
        W2s = _stack_expert_params(W2)
        b2s = _stack_expert_params(b2)
        pre = jnp.einsum('bsh,ehf->besf', x, W1s) + b1s[None, :, None, :]
        act = jax.nn.gelu(pre)
        y = jnp.einsum('besf,efh->besh', act, W2s) + b2s[None, :, None, :]
        out = jnp.einsum('bse,besh->bsh', probs, y)
        return out
    x = x + _L0_xattn_ref(_layernorm(x, axis=-1), ctx_1024, ctx_1024, mask_Bx1xSxS2_bf0, L0_xattn_Wq, L0_xattn_Wo, L0_xattn_W1, L0_xattn_b1, L0_xattn_W2, L0_xattn_b2, L0_xattn_g1, L0_xattn_be1, L0_xattn_g2, L0_xattn_be2)
    x = x + _L0_ffn_ref(_layernorm(x, axis=-1), L0_ffn_gate_w, L0_ffn_gate_b, L0_ffn_expert_w, L0_ffn_expert_b)
    x = x + _L1_xattn_ref(_layernorm(x, axis=-1), ctx_1024, ctx_1024, fside_Bx1xSxS2_0, L1_xattn_Wq, L1_xattn_Wk, L1_xattn_Wv, L1_xattn_Wo, 16)
    x = x + _L1_ffn_ref(_layernorm(x, axis=-1), L1_ffn_W1, L1_ffn_b1, L1_ffn_W2, L1_ffn_b2, L1_ffn_ln_gamma, L1_ffn_ln_beta, L1_ffn_Wr, L1_ffn_br)
    return x

_drawn_inputs = setup_inputs


def setup_inputs(seed=0):
    import zlib

    import numpy as np

    out = dict(_drawn_inputs(seed))
    spreads = {'L0_xattn_b1': (0.0, 0.1),
     'L0_xattn_b2': (0.0, 0.1),
     'L0_xattn_g1': (1.0, 0.2),
     'L0_xattn_be1': (0.0, 0.1),
     'L0_xattn_g2': (1.0, 0.2),
     'L0_xattn_be2': (0.0, 0.1),
     'L0_ffn_gate_b': (0.0, 0.1),
     'L0_ffn_expert_b': (0.0, 0.1),
     'L1_ffn_ln_gamma': (1.0, 0.6),
     'L1_ffn_ln_beta': (0.0, 0.8),
     'L1_ffn_br': (0.0, 0.8)}
    factors = {'L1_ffn_b1': 8.0, 'L1_ffn_b2': 8.0, 'L1_ffn_Wr': 3.002}
    for name, (base, spread) in spreads.items():
        noise = np.random.default_rng([zlib.crc32(name.encode()), seed]).standard_normal(out[name].shape)
        drawn = base * np.exp(spread * noise) if base else spread * noise
        out[name] = jnp.asarray(drawn.astype(out[name].dtype))
    for name, factor in factors.items():
        out[name] = (out[name] * factor).astype(out[name].dtype)
    return out
```

```python
from contextlib import ExitStack

import concourse.bass as bass
from concourse import mybir

ALU = mybir.AluOpType
ACT = mybir.ActivationFunctionType
AX = mybir.AxisListType.X
F32 = mybir.dt.float32
BF16 = mybir.dt.bfloat16
I32 = mybir.dt.int32
U8 = mybir.dt.uint8

P = 128
EPS = 1e-5
FAR = -3.0e38


def plan_products(TILES, HALVES, ROUNDS):
    plan = []

    def big(key, drain):
        plan.append((key, "big", drain))

    def small(key, drain):
        plan.append((key, "small", drain))

    rounds = iter(range(ROUNDS))

    def count():
        r = next(rounds, None)
        if r is not None:
            small(("count", r), "dve")

    small(("w0_T",), "act")
    big(("ctx_T",), "act")
    big(("xn_T", "attn0"), "act")
    for name in ("k0", "q0"):
        big((name,), "act")
    big(("ffn0_w_T",), "act")
    big(("expert_w_T",), "act")
    big(("wo1_T",), "act")
    for part in range(2):
        big(("qk_weight", part), "act")
        big(("vo_weight", part), "act")
    for i in range(TILES + 4):
        if i < TILES:
            small(("v0", i), "dve")
            big(("scores0", i), "dve")
        if 1 <= i <= TILES:
            big(("probs0_T", i - 1), "act")
        if 2 <= i < TILES + 2:
            small(("attended0", i - 2), "dve")
            count()
        if 3 <= i < TILES + 3:
            small(("attended0_T", i - 3), "act")
        if 4 <= i < TILES + 4:
            small(("project0", i - 4), "dve")
    for g in range(HALVES):
        small(("x1_T", g), "act")
    for g in range(HALVES):
        for f in range(0, 4, 2):
            big(("ffn0_up", g, f), "act")
    for g in range(HALVES):
        small(("ffn0_down", g), "dve")
        for _ in range(3):
            count()
    for h in range(5):
        big(("keys1", h), "act")
    big(("xn_T", "experts"), "act")
    small(("gate",), "dve")
    for t in range(TILES):
        big(("experts", t), "act")
        big(("keys1", 5 + t), "act")
        count()
    for h in range(5 + TILES, 16):
        big(("keys1", h), "act")
    big(("xn_T", "attn1"), "act")
    for i in range(TILES + 2):
        if i < TILES:
            big(("scores1", i), "dve")
            big(("values1", i, 0), "act")
            big(("values1", i, 1), "act")
        if 1 <= i <= TILES:
            big(("probs1_T", i - 1), "act")
        if 2 <= i:
            small(("attended1", i - 2), "dve")
            count()
    count()
    assert next(rounds, None) is None
    big(("xn_T", "moe"), "act")
    big(("router_T",), "act")
    small(("router",), "dve")
    small(("limits",), "dve")
    for g in range(HALVES):
        for e in range(2):
            for f in range(0, 4, 2):
                big(("moe_up", g, e, f), "act")
            small(("moe_down", g, e), "dve")
    return plan


class Rings:

    SLOTS = {"big": 3, "small": 2}

    def __init__(self, plan):
        self.plan = plan
        self.slot, self.filled, self.drained, self.before = {}, {}, {}, {}
        order = {"big": [], "small": []}
        drains = {"act": 0, "dve": 0}
        for key, ring, drain in plan:
            n = len(order[ring])
            self.slot[key] = (ring, n % self.SLOTS[ring])
            self.filled[key] = (ring, n + 1)
            self.before[key] = order[ring][n - self.SLOTS[ring]] if n >= self.SLOTS[ring] else None
            order[ring].append(key)
            drains[drain] += 1
            self.drained[key] = (drain, drains[drain])


def build(nc, a, out):
    B, S, D = a["x"].shape
    TOK = B * S
    TILES = TOK // P
    HALVES = 2
    TH = TILES // HALVES
    TC = TH * P
    H = 16
    HP = H // 2
    DK0 = D // H
    DK1 = a["L1_xattn_Wq"].shape[0] // H
    E = a["L0_ffn_gate_w"].shape[0]
    F = a["L0_xattn_W1"].shape[0]
    FC = F // P
    KEYS = a["ctx_1024"].shape[1]
    SCALE0 = 1.0 / float(D) ** 0.5
    SPARSITY, GAIN = 0.1, 0.8
    sizes = [F * D, F * D, F, D]
    low = [max(1, int(n * SPARSITY / 2)) for n in sizes]
    high = [n - k + 1 for n, k in zip(sizes, low)]
    BITS = 31
    assert S == 64 and KEYS == 64 and D == P and DK1 == 64 and F == 4 * P and E == 8

    plan = plan_products(TILES, HALVES, BITS)
    rings = Rings(plan)

    with ExitStack() as ctx:
        def sb(name, shape, dt=F32):
            return ctx.enter_context(nc.sbuf_tensor(name, shape, dt))

        named = {}

        def sem(name):
            if name not in named:
                named[name] = ctx.enter_context(nc.semaphore(name))
            return named[name]

        xt = sb("xt", [P, TILES, D])
        ctx_tok = sb("ctx_tok", [P, TILES, D])
        fside = sb("fside", [P, TILES, KEYS])
        mask_in = sb("mask_in", [P, TILES, KEYS], U8)
        mask_add = sb("mask_add", [P, TILES, KEYS])
        wq0 = sb("wq0", [P, D])
        wo0 = sb("wo0", [P, D])
        w1_0 = sb("w1_0", [P, FC, D])
        w2_0 = sb("w2_0", [P, F])
        b1_rows = sb("b1_rows", [2 * FC, P])
        b1_cols = sb("b1_cols", [P, 2 * FC])
        b1_0, b1_1 = b1_cols[:, 0:FC], b1_cols[:, FC:2 * FC]
        rows = {n: sb(n, [P, D]) for n in ("row_b2", "row_g1", "row_be1", "row_g2", "row_be2", "row_gamma",
                                           "row_beta", "row_y0", "row_y1")}
        gate_w = sb("gate_w", [E, D])
        row_gate_b = sb("row_gate_b", [P, E])
        row_br = sb("row_br", [P, E])
        expert_w = sb("expert_w", [P, E, D])
        expert_b = sb("expert_b", [1, E * D])
        raw1 = sb("raw1", [P, 4, HP, D])
        wq1, wk1, wv1, wo1 = (raw1[:, i] for i in range(4))
        w1_1 = sb("w1_1", [P, F])
        w2_1 = sb("w2_1", [P, FC, D])
        wr = sb("wr", [P, E])
        ranked_w = sb("ranked_w", [P, F * D // 32])
        ranked_b = sb("ranked_b", [P, F // 32])
        below = sb("below", [P, F * D // 32], BF16)
        below_b = sb("below_b", [P, F // 32], BF16)

        ident = sb("ident", [P, P])
        ones = sb("ones", [P, P])
        groups = sb("groups", [P, P])
        head_mask = sb("head_mask", [P, H])
        pair_mask = sb("pair_mask", [P, HP, 2, DK0])
        half_exp = sb("half_exp", [P, TILES])

        wq0_T = sb("wq0_T", [P, D])[:]
        wo0_T = sb("wo0_T", [P, D])
        gate_w_T = sb("gate_w_T", [P, E])
        w1_0T = sb("w1_0T", [P, F])
        w2_0T = sb("w2_0T", [P, FC, D])
        expert_w_T = sb("expert_w_T", [P, E, D])
        qk_w = sb("qk_w", [P, H, D])
        vo_w = sb("vo_w", [P, H, D])
        w1_p = w1_0[:].rearrange("p c d -> p (c d)")
        w2_p = w2_0[:].rearrange("p (c d) -> p c d", c=FC)
        b1_p = sb("b1_p", [P, FC])

        xn = sb("xn", [P, TILES, D])
        xn_T = sb("xn_T", [P, TOK])
        ctx_T = sb("ctx_T", [P, TOK])
        head_keys = sb("head_keys", [P, H, TOK])
        v0 = sb("v0", [P, 2, 2, D])
        work = sb("work", [P, 2, H, KEYS])
        probs_T = sb("probs_T", [P, 2, HP, P])
        wo1_T = probs_T[:, 0]
        att = sb("att", [P, 2, D])
        att_T = sb("att_T", [P, 2, D])
        values1 = sb("values1", [P, 2, 2, HP, D])
        q0_T = values1[:, 0, 0].rearrange("p h d -> p (h d)")
        k0_T = values1[:, 0, 1].rearrange("p h d -> p (h d)")
        hidden = raw1[:].rearrange("p a h d -> p (a h d)").rearrange("p (e f t) -> p e f t", e=2, f=FC)
        row_max = sb("row_max", [P, 2, H])
        row_sum = sb("row_sum", [P, 2, H])
        row_inv = sb("row_inv", [P, 2, H])
        stats = sb("stats", [P, TILES, 6])
        moments = sb("moments", [P, TILES, 2])
        var_eps = sb("var_eps", [P, TILES])
        rstd = sb("rstd", [P, TILES])
        res = ctx_tok
        x1 = expert_w
        pooled_T = sb("pooled_T", [P, B])
        logits = sb("logits", [P, TILES, E])
        best = sb("best", [P, TILES, 8])
        weights = sb("weights", [P, TILES, E])
        kept = sb("kept", [P, TILES, E])
        total = sb("total", [P, TILES])
        gates = sb("gates", [P, TILES, E])
        share = sb("share", [P, TILES, 2])
        limit = sb("limit", [P, 2], I32)
        tried = sb("tried", [P, 2], I32)
        counted = sb("counted", [P, 2])
        rank = sb("rank", [P, 2])
        keep_bit = sb("keep_bit", [P, 2], I32)
        picks = sb("picks", [P, 4])
        picked = sb("picked", [P, 2, 4])
        limits = sb("limits", [P, 2, 4])
        size, tier, tier2 = (head_keys[:, h, 0:F] for h in range(3))

        big = [ctx.enter_context(nc.psum_tensor(f"big{i}", [P, 2, 512], F32)) for i in range(3)]
        small = [ctx.enter_context(nc.psum_tensor(f"small{i}", [P, 512], F32)) for i in range(2)]

        def psum(key):
            ring, n = rings.slot[key]
            return big[n] if ring == "big" else small[n]

        def wait_filled(eng, key):
            ring, n = rings.filled[key]
            eng.wait_ge(sem(f"{ring}_filled"), n)

        def wait_drained(eng, key):
            who, n = rings.drained[key]
            eng.wait_ge(sem(f"{who}_drained"), n)

        for name in ("big_filled", "small_filled", "act_drained", "dve_drained"):
            sem(name)

        tok = lambda ap: ap.rearrange("(t b) s d -> (b s) t d", b=2)
        LOADS = [
            ("x", xt[:], tok(a["x"])),
            ("ctx", ctx_tok[:], tok(a["ctx_1024"])),
            ("w0", wq0[:], a["L0_xattn_Wq"]),
            ("w0", wo0[:], a["L0_xattn_Wo"]),
            ("w0", gate_w[:], a["L0_ffn_gate_w"]),
            ("w0", b1_rows[0:FC], a["L0_xattn_b1"].rearrange("(c p) -> c p", p=P)),
            ("w0", b1_rows[FC:2 * FC], a["L1_ffn_b1"].rearrange("(c p) -> c p", p=P)),
            ("mask", mask_in[:], a["mask_Bx1xSxS2_bf0"].rearrange("(t b) o s k -> (b o s) t k", b=2)),
            ("ranked", ranked_w[0:32], a["L1_ffn_W1"].rearrange("(p r) f -> p (r f)", p=32)),
            ("ranked", ranked_w[32:64], a["L1_ffn_W1"].rearrange("(p r) f -> p (r f)", p=32)),
            ("ranked", ranked_w[64:96], a["L1_ffn_W2"].rearrange("(p r) f -> p (r f)", p=32)),
            ("ranked", ranked_w[96:128], a["L1_ffn_W2"].rearrange("(p r) f -> p (r f)", p=32)),
            ("ranked", ranked_b[0:32], a["L1_ffn_b1"].rearrange("(p r) -> p r", p=32)),
            ("ranked", ranked_b[32:64], a["L1_ffn_b1"].rearrange("(p r) -> p r", p=32)),
            ("ranked_b2", ranked_b[64:96, 0:D // 32], a["L1_ffn_b2"].rearrange("(p r) -> p r", p=32)),
            ("ranked_b2", ranked_b[96:128, 0:D // 32], a["L1_ffn_b2"].rearrange("(p r) -> p r", p=32)),
            ("ffn0_w", w1_0[:], a["L0_xattn_W1"].rearrange("(c p) d -> p c d", p=P)),
            ("ffn0_w", w2_0[:], a["L0_xattn_W2"]),
            ("expert_w", expert_w[:], a["L0_ffn_expert_w"].rearrange("e o d -> o e d")),
            ("w1", wo1[:].rearrange("p h d -> p (h d)"), a["L1_xattn_Wo"]),
            ("w1", wq1[:], a["L1_xattn_Wq"].rearrange("(h p) d -> p h d", p=P)),
            ("w1", wk1[:], a["L1_xattn_Wk"].rearrange("(h p) d -> p h d", p=P)),
            ("w1", wv1[:], a["L1_xattn_Wv"].rearrange("(h p) d -> p h d", p=P)),
            ("fside", fside[:], a["fside_Bx1xSxS2_0"].rearrange("(t b) o s k -> (b o s) t k", b=2)),
            ("expert_b", expert_b[:], a["L0_ffn_expert_b"].rearrange("(a e) d -> a (e d)", a=1)),
            ("ffn1", w1_1[:], a["L1_ffn_W1"]),
            ("ffn1", w2_1[:], a["L1_ffn_W2"].rearrange("(c p) d -> p c d", p=P)),
            ("ffn1", wr[:], a["L1_ffn_Wr"]),
        ] + [("rows", t[:], a[n].partition_broadcast(P)) for t, n in (
            (rows["row_b2"], "L0_xattn_b2"), (rows["row_g1"], "L0_xattn_g1"), (rows["row_be1"], "L0_xattn_be1"),
            (rows["row_g2"], "L0_xattn_g2"), (rows["row_be2"], "L0_xattn_be2"), (rows["row_gamma"], "L1_ffn_ln_gamma"),
            (rows["row_beta"], "L1_ffn_ln_beta"), (rows["row_y0"], "L1_ffn_b2"), (row_gate_b, "L0_ffn_gate_b"),
            (row_br, "L1_ffn_br"))]
        loaded = {}
        for name, _, _ in LOADS:
            loaded[name] = loaded.get(name, 0) + 16
            sem(f"loaded_{name}")

        def wait_loaded(eng, name):
            eng.wait_ge(sem(f"loaded_{name}"), loaded[name])

        block = ctx.enter_context(nc.Block())

        @block.sync
        def _(sp):
            for name, dst, src in LOADS:
                if name == "ranked_b2":
                    sp.wait_ge(sem("bias_padded"), 1)
                sp.dma_start(dst, src).then_inc(sem(f"loaded_{name}"), 16)
            out_tok = tok(out)
            for g in range(HALVES):
                sp.wait_ge(sem("x_done"), TH * (g + 1))
                sp.dma_start(out_tok[:, g * TH:(g + 1) * TH], xt[:, g * TH:(g + 1) * TH]).then_inc(sem("stored"), 16)
            sp.wait_ge(sem("stored"), 16 * HALVES)

        @block.gpsimd
        def _(pool):
            nc.gpsimd.memset(ident[:], 0.0).then_inc(sem("pool_step"), 1)
            nc.gpsimd.memset(half_exp[:], -0.5).then_inc(sem("pool_step"), 1)
            nc.gpsimd.memset(head_mask[:], 1.0).then_inc(sem("pool_step"), 1)
            pool.wait_ge(sem("pool_step"), 3)
            nc.gpsimd.affine_select(out=ident[:], in_=ident[:], compare_op=ALU.not_equal, fill=1.0, base=0,
                                    pattern=[[-1, P]], channel_multiplier=1).then_inc(sem("ident_ready"), 1)
            nc.gpsimd.affine_select(out=head_mask[:], in_=head_mask[:], compare_op=ALU.is_ge, fill=0.0, base=0,
                                    pattern=[[-DK0, H]], channel_multiplier=1).then_inc(sem("pool_step"), 1)
            pool.wait_ge(sem("pool_step"), 4)
            nc.gpsimd.affine_select(out=head_mask[:], in_=head_mask[:], compare_op=ALU.is_ge, fill=0.0, base=DK0 - 1,
                                    pattern=[[DK0, H]], channel_multiplier=-1).then_inc(sem("masks_ready"), 1)

            def inverse_root(n):
                pool.wait_ge(sem("var_ready"), n + 1)
                nc.gpsimd.tensor_tensor(rstd[:], var_eps[:], half_exp[:], ALU.pow).then_inc(sem("rstd_ready"), 1)

            def subtract_max(layer, t):
                pool.wait_ge(sem(f"max{layer}_ready"), t + 1)
                nc.gpsimd.tensor_tensor(work[:, t % 2], work[:, t % 2],
                                        row_max[:, t % 2].unsqueeze(2).broadcast_to([P, H, KEYS]),
                                        ALU.subtract).then_inc(sem(f"shifted{layer}"), 1)

            inverse_root(0)
            for t in range(TILES):
                subtract_max(0, t)
            for n in range(1, 5):
                inverse_root(n)
            for t in range(TILES):
                subtract_max(1, t)
            inverse_root(5)
            inverse_root(6)

        @block.scalar
        def _(act):
            def drain(dst, key, src=None, func=ACT.Copy, last=True, **kw):
                wait_filled(act, key)
                ins = nc.scalar.activation(dst, psum(key)[:] if src is None else src, func, **kw)
                if last:
                    ins.then_inc(sem("act_drained"), 1)

            def two(ap):
                return ap.rearrange("p (a n) -> p a n", a=2)

            key = ("w0_T",)
            ps = psum(key)
            drain(wq0_T, key, ps[:, 0:D], last=False)
            drain(wo0_T[:], key, ps[:, D:2 * D], last=False)
            drain(gate_w_T[:], key, ps[:, 2 * D:2 * D + E], last=False)
            drain(b1_cols[:], key, ps[:, 3 * D:3 * D + 2 * FC])
            drain(two(ctx_T[:]), ("ctx_T",))
            drain(two(xn_T[:]), ("xn_T", "attn0"))
            drain(two(k0_T), ("k0",))
            drain(two(q0_T), ("q0",))
            drain(w1_0T[:], ("ffn0_w_T",), psum(("ffn0_w_T",))[:, 0], last=False)
            drain(w2_0T[:].rearrange("p c d -> p (c d)"), ("ffn0_w_T",), psum(("ffn0_w_T",))[:, 1])
            drain(two(expert_w_T[:].rearrange("p e d -> p (e d)")), ("expert_w_T",))
            drain(two(wo1_T.rearrange("p h d -> p (h d)")), ("wo1_T",))
            for part in range(2):
                half = slice(part * HP, part * HP + HP)
                for dst, key in ((qk_w, ("qk_weight", part)), (vo_w, ("vo_weight", part))):
                    drain(dst[:, half].rearrange("p (h w) d -> p w h d", w=2), key,
                          psum(key)[:].rearrange("p w (h d) -> p w h d", d=D))

            def exponentials(layer, t):
                act.wait_ge(sem(f"shifted{layer}"), t + 1)
                nc.scalar.activation(work[:, t % 2], work[:, t % 2], ACT.Exp).then_inc(sem(f"exp{layer}"), 1)

            def probs_out(layer, t):
                if t >= 2:
                    wait_filled(act, (f"attended{layer}", t - 2))
                drain(two(probs_T[:, t % 2].rearrange("p h q -> p (h q)")), (f"probs{layer}_T", t))

            for i in range(TILES + 4):
                if i < TILES:
                    exponentials(0, i)
                if 1 <= i <= TILES:
                    probs_out(0, i - 1)
                if 3 <= i < TILES + 3:
                    drain(att_T[:, (i - 3) % 2], ("attended0_T", i - 3), psum(("attended0_T", i - 3))[:, 0:D])
            for g in range(HALVES):
                drain(xn_T[:, g * TC:(g + 1) * TC], ("x1_T", g))
            wait_drained(act, ("vo_weight", 1))
            for g in range(HALVES):
                for f in range(0, FC, 2):
                    key = ("ffn0_up", g, f)
                    for j in range(2):
                        drain(hidden[:, g, f + j], key, psum(key)[:, j], ACT.Gelu, last=(j == 1),
                              bias=b1_0[:, f + j:f + j + 1])

            def keys_out(h):
                drain(two(head_keys[:, h]), ("keys1", h))

            def gate_exponentials(n):
                act.wait_ge(sem("gate_shifted"), n)
                nc.scalar.activation(weights[:], weights[:], ACT.Exp).then_inc(sem("gate_exp"), 1)

            for h in range(5):
                keys_out(h)
            drain(two(xn_T[:]), ("xn_T", "experts"))
            gate_exponentials(1)
            for t in range(TILES):
                if t >= 2:
                    act.wait_ge(sem("expert_added"), t - 1)
                drain(two(work[:, t % 2].rearrange("p h k -> p (h k)")), ("experts", t), func=ACT.Gelu)
                keys_out(5 + t)
            for h in range(5 + TILES, H):
                keys_out(h)
            drain(two(xn_T[:]), ("xn_T", "attn1"))
            for i in range(TILES + 2):
                if i < TILES:
                    for b in range(2):
                        if i >= 2 and b == 0:
                            wait_filled(act, ("attended1", i - 2))
                        drain(two(values1[:, i % 2, b].rearrange("p h d -> p (h d)")), ("values1", i, b))
                    exponentials(1, i)
                if 1 <= i <= TILES:
                    probs_out(1, i - 1)
            drain(two(xn_T[:]), ("xn_T", "moe"))
            drain(two(ctx_T[:]), ("router_T",))
            gate_exponentials(2)
            wait_loaded(act, "ffn1")
            for g in range(HALVES):
                for e in range(2):
                    if e == 1 and g == 0:
                        act.wait_ge(sem("bias_perturbed"), 1)
                    if g == 1:
                        wait_filled(act, ("moe_down", 0, e))
                    for f in range(0, FC, 2):
                        key = ("moe_up", g, e, f)
                        for j in range(2):
                            drain(hidden[:, e, f + j], key, psum(key)[:, j], ACT.Gelu_apprx_tanh, last=(j == 1),
                                  bias=(b1_1 if e == 0 else b1_p)[:, f + j:f + j + 1])

        @block.vector
        def _(dve):
            V = nc.vector
            steps = [0]

            def step(ins):
                steps[0] += 1
                ins.then_inc(sem("dve_step"), 1)
                return steps[0]

            def after(n):
                dve.wait_ge(sem("dve_step"), n)

            def drained(ins):
                ins.then_inc(sem("dve_drained"), 1)

            V.memset(ones[:], 1.0).then_inc(sem("ones_ready"), 1)
            n = step(V.memset(groups[:], 0.0))
            n = step(V.memset(pair_mask[:], 0.0))
            n = step(V.memset(mask_add[:], 0.0))
            n = step(V.memset(work[:, 0], FAR))
            V.memset(ranked_b[64:128], 3.0e38).then_inc(sem("bias_padded"), 1)
            n = step(V.memset(limit[:], 0))
            for g in range(4):
                n = step(V.memset(rank[32 * g:32 * g + 32, 0:1], float([low, high][g % 2][g // 2] - 1)))
                n = step(V.memset(rank[32 * g:32 * g + 32, 1:2], float([low, high][g % 2][2 + g // 2] - 1)))
            after(n)
            for g in range(4):
                n = step(V.memset(groups[32 * g:32 * g + 32, 32 * g:32 * g + 32], 1.0))
            for h2 in range(2):
                n = step(V.memset(pair_mask[64 * h2:64 * h2 + 64, :, h2], 1.0))
            n = step(V.memset(picks[:], 0.0))
            after(n)
            for g in range(4):
                n = step(V.memset(picks[32 * g:32 * g + 1, g:g + 1], 1.0))

            norms = [0]

            def layer_norm(src, tiles, write, gain=None, shift=None, dst=None):
                k = norms[0]
                norms[0] += 1
                for t in tiles:
                    m = step(V.bn_stats(stats[:, t], src[:, t]))
                after(m)
                for t in tiles:
                    m = step(V.bn_aggr(moments[:, t], stats[:, t]))
                after(m)
                V.tensor_scalar(var_eps[:], moments[:, :, 1], EPS, None, ALU.add).then_inc(sem("var_ready"), 1)
                dve.wait_ge(sem("rstd_ready"), k + 1)
                for t in tiles:
                    ins = V.tensor_scalar(dst[:, t], src[:, t], moments[:, t, 0:1], rstd[:, t:t + 1],
                                          ALU.subtract, ALU.mult)
                    if gain is None:
                        ins.then_inc(sem(write), 1)
                    else:
                        m = step(ins)
                if gain is not None:
                    after(m)
                    whole = lambda r: r[:].unsqueeze(1).broadcast_to([P, TILES, D])
                    m = step(V.tensor_tensor(dst[:], dst[:], whole(gain), ALU.mult))
                    after(m)
                    V.tensor_tensor(dst[:], dst[:], whole(shift), ALU.add).then_inc(sem(write), 1)

            def try_bit(r):
                bit = 1 << (BITS - 1 - r)
                if r >= 1:
                    dve.wait_ge(sem("limit_kept"), r)
                m = step(V.tensor_scalar(tried[:], limit[:], bit, None, ALU.bitwise_or))
                after(m)
                if r >= 1:
                    wait_filled(dve, ("count", r - 1))
                V.tensor_scalar(below[:], ranked_w[:], tried[:, 0:1].bitcast(F32), None, ALU.is_lt, ALU.add,
                                accum_out=counted[:, 0:1]).then_inc(sem("counted"), 1)
                V.tensor_scalar(below_b[:], ranked_b[:], tried[:, 1:2].bitcast(F32), None, ALU.is_lt, ALU.add,
                                accum_out=counted[:, 1:2]).then_inc(sem("counted"), 1)

            def keep_or_not(r):
                key = ("count", r)
                wait_filled(dve, key)
                drained(V.tensor_tensor(keep_bit[:], psum(key)[:, 0:2], rank[:], ALU.is_le))
                wait_drained(dve, key)
                V.copy_predicated(limit[:], keep_bit[:], tried[:]).then_inc(sem("limit_kept"), 1)

            next_round = [0]

            def count_round():
                r = next_round[0]
                if r > BITS:
                    return
                if r >= 1:
                    keep_or_not(r - 1)
                if r < BITS:
                    try_bit(r)
                next_round[0] += 1

            wait_loaded(dve, "x")
            layer_norm(xt, range(TILES), "xn_attn0", dst=xn)
            wait_loaded(dve, "mask")
            n = step(V.copy_predicated(mask_add[:], mask_in[:], work[:, 0, 0:TILES]))
            mask_step = n
            wait_drained(dve, ("k0",))
            dve.wait_ge(sem("masks_ready"), 1)
            for h in range(H):
                V.tensor_scalar(head_keys[:, h], k0_T, head_mask[:, h:h + 1], None,
                                ALU.mult).then_inc(sem("head_keys0"), 1)
            wait_loaded(dve, "ranked")
            wait_loaded(dve, "ranked_b2")
            n = step(V.tensor_scalar(ranked_w[:].bitcast(I32), ranked_w[:].bitcast(I32), 0x7FFFFFFF, None,
                                     ALU.bitwise_and))
            n = step(V.tensor_scalar(ranked_b[:].bitcast(I32), ranked_b[:].bitcast(I32), 0x7FFFFFFF, None,
                                     ALU.bitwise_and))
            after(n)
            count_round()

            heads = lambda ap: ap.rearrange("p a (h k) -> p (a h) k", k=KEYS)

            def scores_in(layer, t):
                key = (f"scores{layer}", t)
                wait_filled(dve, key)
                if t >= 2:
                    wait_filled(dve, (f"probs{layer}_T", t - 2))
                added = (mask_add if layer == 0 else fside)[:, t].unsqueeze(1).broadcast_to([P, H, KEYS])
                drained(V.scalar_tensor_tensor(out=work[:, t % 2], in0=heads(psum(key)[:]),
                                               scalar=SCALE0 if layer == 0 else 1.0, in1=added,
                                               op0=ALU.mult, op1=ALU.add))
                wait_drained(dve, key)
                V.tensor_reduce(row_max[:, t % 2], work[:, t % 2], AX, ALU.max).then_inc(sem(f"max{layer}_ready"), 1)

            def sums(layer, t):
                dve.wait_ge(sem(f"exp{layer}"), t + 1)
                m = step(V.tensor_reduce(row_sum[:, t % 2], work[:, t % 2], AX, ALU.add))
                after(m)
                return step(V.reciprocal(row_inv[:, t % 2], row_sum[:, t % 2]))

            def attended0(t, inv):
                key = ("attended0", t)
                wait_filled(dve, key)
                if t >= 2:
                    wait_filled(dve, ("attended0_T", t - 2))
                after(inv)
                for b in range(2):
                    rows_b = slice(S * b, S * b + S)
                    src = psum(key)[rows_b, 0:2 * D].rearrange("p (c b w d) -> p c b w d", b=2, w=2, d=DK0)
                    inv_b = row_inv[rows_b, t % 2].rearrange("p (c w) -> p c w", w=2).unsqueeze(3)
                    ins = V.tensor_tensor(att[rows_b, t % 2].rearrange("p (c w d) -> p c w d", w=2, d=DK0),
                                          src[:, :, b], inv_b.broadcast_to([S, HP, 2, DK0]), ALU.mult)
                    if b == 1:
                        drained(ins)
                    else:
                        step(ins)

            invs = {}
            after(mask_step)
            wait_drained(dve, ("k0",))
            for i in range(TILES + 4):
                if i < TILES:
                    key = ("v0", i)
                    wait_filled(dve, key)
                    if i >= 2:
                        wait_filled(dve, ("attended0", i - 2))
                    drained(V.tensor_tensor(v0[:, i % 2], psum(key)[:, 0:2 * D].rearrange("p (b d) -> p b d", b=2),
                                            pair_mask[:].rearrange("p a b c -> p (a b c)").unsqueeze(1)
                                            .broadcast_to([P, 2, D]), ALU.mult))
                    scores_in(0, i)
                if 1 <= i <= TILES:
                    invs[i - 1] = sums(0, i - 1)
                if 2 <= i < TILES + 2:
                    attended0(i - 2, invs[i - 2])
                    count_round()
                if 4 <= i:
                    t = i - 4
                    wait_filled(dve, ("project0", t))
                    drained(V.tensor_tensor(res[:, t], psum(("project0", t))[:, 0:D], xn[:, t], ALU.add))
            wait_drained(dve, ("project0", TILES - 1))
            wait_loaded(dve, "rows")
            layer_norm(res, range(TILES), "x1_ready", rows["row_g1"], rows["row_be1"], x1)
            dve.wait_ge(sem("x1_ready"), 1)
            for g in range(HALVES):
                key = ("ffn0_down", g)
                wait_filled(dve, key)
                drained(V.tensor_tensor(res[:, g * TH:g * TH + TH], psum(key)[:].rearrange("p (t d) -> p t d", t=TH),
                                        x1[:, g * TH:g * TH + TH], ALU.add))
                for _ in range(3):
                    count_round()
            wait_drained(dve, ("ffn0_down", HALVES - 1))
            n = step(V.tensor_tensor(res[:], res[:], rows["row_b2"][:].unsqueeze(1).broadcast_to([P, TILES, D]),
                                     ALU.add))
            after(n)
            layer_norm(res, range(TILES), "ffn0_ready", rows["row_g2"], rows["row_be2"], x1)
            dve.wait_ge(sem("ffn0_ready"), 1)
            n = step(V.tensor_tensor(xt[:], xt[:], x1[:], ALU.add))
            after(n)

            layer_norm(xt, range(TILES), "xn_experts", dst=xn)
            wait_drained(dve, ("xn_T", "experts"))
            after(step(V.tensor_reduce(pooled_T[:], xn_T[:].rearrange("p (b s) -> p b s", s=S), AX, ALU.add)))
            V.tensor_copy(xn[:].rearrange("p t (b s) -> p (t b) s", b=2),
                          pooled_T[:].unsqueeze(2).broadcast_to([P, B, S])).then_inc(sem("pooled"), 1)
            key = ("gate",)
            wait_filled(dve, key)
            drained(V.scalar_tensor_tensor(out=logits[:], in0=psum(key)[:, 0:TILES * E].rearrange("p (t e) -> p t e", e=E),
                                           scalar=1.0 / S, in1=row_gate_b[:].unsqueeze(1).broadcast_to([P, TILES, E]),
                                           op0=ALU.mult, op1=ALU.add))
            wait_drained(dve, key)
            for t in range(TILES):
                n = step(V.max(best[:, t], logits[:, t]))
            after(n)
            wide = lambda ap: ap.broadcast_to([P, TILES, E])
            V.tensor_tensor(weights[:], logits[:], wide(best[:, :, 0:1]), ALU.subtract).then_inc(sem("gate_shifted"), 1)
            n = step(V.tensor_tensor(kept[:], logits[:], wide(best[:, :, 1:2]), ALU.is_ge))

            def weigh(n_exp, masked, n):
                dve.wait_ge(sem("gate_exp"), n_exp)
                after(n)
                if masked:
                    m = step(V.tensor_tensor(weights[:], weights[:], kept[:], ALU.mult))
                    after(m)
                m = step(V.tensor_reduce(total[:], weights[:], AX, ALU.add))
                after(m)
                m = step(V.reciprocal(total[:], total[:]))
                after(m)
                m = step(V.tensor_tensor(gates[:], weights[:], wide(total[:].unsqueeze(2)), ALU.mult))
                after(m)

            weigh(1, True, n)
            for t in range(TILES):
                wait_drained(dve, ("experts", t))
                out_e = work[:, t % 2].rearrange("p h k -> p (h k)").rearrange("p (e d) -> p e d", e=E)
                for e in range(E):
                    ins = V.scalar_tensor_tensor(out=xt[:, t], in0=out_e[:, e], scalar=gates[:, t, e:e + 1],
                                                 in1=xt[:, t], op0=ALU.mult, op1=ALU.add)
                    if e < E - 1:
                        after(step(ins))
                    else:
                        ins.then_inc(sem("expert_added"), 1)
                count_round()
            dve.wait_ge(sem("expert_added"), TILES)

            layer_norm(xt, range(TILES), "xn_attn1", dst=xn)
            wait_loaded(dve, "fside")
            for i in range(TILES + 2):
                if i < TILES:
                    scores_in(1, i)
                if 1 <= i <= TILES:
                    t = i - 1
                    after(sums(1, t))
                    V.tensor_tensor(work[:, t % 2], work[:, t % 2],
                                    row_inv[:, t % 2].unsqueeze(2).broadcast_to([P, H, KEYS]),
                                    ALU.mult).then_inc(sem("probs1"), 1)
                if 2 <= i:
                    t = i - 2
                    wait_filled(dve, ("attended1", t))
                    drained(V.tensor_tensor(xt[:, t], psum(("attended1", t))[:, 0:D], xt[:, t], ALU.add))
                    count_round()
            wait_drained(dve, ("attended1", TILES - 1))

            layer_norm(xt, range(TILES), "xn_moe", dst=xn)
            dve.wait_ge(sem("xn_moe"), TILES)
            layer_norm(xn, range(TILES), "router_in", rows["row_gamma"], rows["row_beta"], x1)
            while next_round[0] <= BITS:
                count_round()
            dve.wait_ge(sem("limit_kept"), BITS)
            for j in range(2):
                V.tensor_scalar(picked[:, j], picks[:], limit[:, j:j + 1].bitcast(F32), None,
                                ALU.mult).then_inc(sem("picked"), 1)
            key = ("router",)
            wait_filled(dve, key)
            drained(V.tensor_tensor(logits[:], psum(key)[:, 0:TILES * E].rearrange("p (t e) -> p t e", e=E),
                                    row_br[:].unsqueeze(1).broadcast_to([P, TILES, E]), ALU.add))
            wait_drained(dve, key)
            n = step(V.tensor_reduce(total[:], logits[:], AX, ALU.max))
            after(n)
            V.tensor_tensor(weights[:], logits[:], wide(total[:].unsqueeze(2)), ALU.subtract)\
             .then_inc(sem("gate_shifted"), 1)
            key = ("limits",)
            wait_filled(dve, key)
            drained(V.tensor_copy(limits[:].rearrange("p a b -> p (a b)"), psum(key)[:, 0:8]))
            wait_drained(dve, key)
            wait_loaded(dve, "ffn1")

            def perturb(src, dst, n, j, w, done):
                lo, hi = limits[:, j, 2 * w:2 * w + 1], limits[:, j, 2 * w + 1:2 * w + 2]
                m = step(V.tensor_scalar(size[:, 0:n].bitcast(I32), src.bitcast(I32), 0x7FFFFFFF, None,
                                         ALU.bitwise_and))
                after(m)
                step(V.tensor_scalar(tier[:, 0:n], size[:, 0:n], hi, None, ALU.is_ge))
                m = step(V.tensor_scalar(tier2[:, 0:n], size[:, 0:n], lo, None, ALU.is_le))
                after(m)
                m = step(V.scalar_tensor_tensor(out=size[:, 0:n], in0=tier[:, 0:n], scalar=1.0, in1=tier2[:, 0:n],
                                                op0=ALU.mult, op1=ALU.is_lt))
                after(m)
                m = step(V.tensor_tensor(tier[:, 0:n], size[:, 0:n], tier[:, 0:n], ALU.subtract))
                after(m)
                m = step(V.scalar_tensor_tensor(out=tier2[:, 0:n], in0=src, scalar=GAIN, in1=tier[:, 0:n],
                                                op0=ALU.mult, op1=ALU.mult))
                after(m)
                V.tensor_tensor(dst, tier2[:, 0:n], src, ALU.add).then_inc(sem(done), 1)
                dve.wait_ge(sem(done), 1)

            perturb(b1_1, b1_p[:], FC, 1, 0, "bias_perturbed")
            perturb(w1_1[:], w1_p, F, 0, 0, "w1_perturbed")
            perturb(w2_1[:].rearrange("p c d -> p (c d)"), w2_p.rearrange("p c d -> p (c d)"), F, 0, 1,
                    "w2_perturbed")
            perturb(rows["row_y0"][:], rows["row_y1"][:], D, 1, 1, "row_perturbed")
            dve.wait_ge(sem("gate_exp"), 2)
            n = step(V.tensor_reduce(share[:, :, 1], weights[:, :, 1:E], AX, ALU.add))
            after(n)
            n = step(V.tensor_tensor(total[:], share[:, :, 1], weights[:, :, 0], ALU.add))
            after(n)
            n = step(V.reciprocal(total[:], total[:]))
            after(n)
            n = step(V.tensor_tensor(share[:, :, 0], weights[:, :, 0], total[:], ALU.mult))
            n = step(V.tensor_tensor(share[:, :, 1], share[:, :, 1], total[:], ALU.mult))
            after(n)
            for g in range(HALVES):
                for e in range(2):
                    key = ("moe_down", g, e)
                    wait_filled(dve, key)
                    drained(V.tensor_tensor(res[:, g * TH:g * TH + TH],
                                            psum(key)[:].rearrange("p (t d) -> p t d", t=TH),
                                            rows[f"row_y{e}"][:].unsqueeze(1).broadcast_to([P, TH, D]), ALU.add))
                    wait_drained(dve, key)
                    for t in range(g * TH, g * TH + TH):
                        ins = V.scalar_tensor_tensor(out=xt[:, t], in0=res[:, t], scalar=share[:, t, e:e + 1],
                                                     in1=xt[:, t], op0=ALU.mult, op1=ALU.add)
                        if e == 0:
                            n = step(ins)
                        else:
                            ins.then_inc(sem("x_done"), 1)
                    after(n)

        @block.tensor
        def _(pe):
            def begin(key):
                if rings.before[key] is not None:
                    wait_drained(pe, rings.before[key])
                return psum(key)

            def end(key, ins):
                ins.then_inc(sem(f"{rings.slot[key][0]}_filled"), 1)

            def flat(ps):
                return ps[:].rearrange("p a n -> p (a n)")

            def transposes(key, sources, sizes=P):
                ps = begin(key)
                dst = flat(ps) if rings.slot[key][0] == "big" else ps[:]
                for j, src in enumerate(sources):
                    rows_in = src.shape[0]
                    ins = nc.tensor.transpose(dst[:, j * P:j * P + rows_in], src, ident[0:rows_in, 0:rows_in])
                end(key, ins)

            def xn_T_product(name):
                pe.wait_ge(sem(f"xn_{name}"), TILES)
                transposes(("xn_T", name), [xn[:, t] for t in range(TILES)])

            def run(key):
                kind = key[0]
                if kind == "w0_T":
                    pe.wait_ge(sem("ident_ready"), 1)
                    pe.wait_ge(sem("ones_ready"), 1)
                    wait_loaded(pe, "w0")
                    transposes(key, [wq0[:], wo0[:], gate_w[:], b1_rows[:]])
                elif kind == "ctx_T":
                    wait_loaded(pe, "ctx")
                    transposes(key, [ctx_tok[:, t] for t in range(TILES)])
                elif kind == "xn_T":
                    xn_T_product(key[1])
                elif kind in ("k0", "q0"):
                    ps = begin(key)
                    wait_drained(pe, ("w0_T",))
                    wait_drained(pe, ("ctx_T",) if kind == "k0" else ("xn_T", "attn0"))
                    src = ctx_T if kind == "k0" else xn_T
                    for g in range(HALVES):
                        ins = nc.tensor.matmul(ps[:, g], wq0_T, src[:, g * TC:g * TC + TC], start=True, stop=True)
                    end(key, ins)
                elif kind == "ffn0_w_T":
                    wait_loaded(pe, "ffn0_w")
                    transposes(key, [w1_0[:, c] for c in range(FC)] + [w2_0[:, c * P:c * P + P] for c in range(FC)])
                elif kind == "expert_w_T":
                    wait_loaded(pe, "expert_w")
                    transposes(key, [expert_w[:, e] for e in range(E)])
                elif kind == "wo1_T":
                    wait_loaded(pe, "w1")
                    transposes(key, [wo1[:, h] for h in range(HP)])
                elif kind in ("qk_weight", "vo_weight"):
                    ps = begin(key)
                    wait_drained(pe, ("wo1_T",))
                    for j in range(HP):
                        h = key[1] * HP + j
                        rows_h = slice(DK1 * (h % 2), DK1 * (h % 2) + DK1)
                        left, right = (wk1, wq1) if kind == "qk_weight" else (wv1, wo1_T)
                        ins = nc.tensor.matmul(ps[:, j % 2, (j // 2) * D:(j // 2) * D + D], left[rows_h, h // 2],
                                               right[rows_h, h // 2], start=True, stop=True)
                    end(key, ins)
                elif kind == "v0":
                    ps = begin(key)
                    for b in range(2):
                        at = (2 * key[1] + b) * KEYS
                        for h2 in range(2):
                            ins = nc.tensor.matmul(ps[KEYS * h2:KEYS * h2 + KEYS, b * D:b * D + D],
                                                   ctx_T[:, at:at + KEYS], wq0_T, start=True, stop=True)
                    end(key, ins)
                elif kind in ("scores0", "scores1"):
                    t = key[1]
                    ps = begin(key)
                    if kind == "scores0":
                        wait_drained(pe, ("q0",))
                        pe.wait_ge(sem("head_keys0"), H)
                        queries = q0_T
                    else:
                        wait_drained(pe, ("xn_T", "attn1"))
                        queries = xn_T
                    for a2 in range(2):
                        for b in range(2):
                            at = (2 * t + b) * KEYS
                            ins = nc.tensor.matmul(ps[S * b:S * b + S, a2], queries[:, at:at + S],
                                                   head_keys[:, a2 * HP:a2 * HP + HP, at:at + KEYS],
                                                   start=True, stop=True)
                    end(key, ins)
                elif kind in ("probs0_T", "probs1_T"):
                    t = key[1]
                    if kind == "probs0_T":
                        pe.wait_ge(sem("exp0"), t + 1)
                    else:
                        pe.wait_ge(sem("probs1"), t + 1)
                    transposes(key, [work[:, t % 2, 2 * h:2 * h + 2].rearrange("p h k -> p (h k)")
                                     for h in range(HP)])
                elif kind == "attended0":
                    t = key[1]
                    ps = begin(key)
                    wait_drained(pe, ("probs0_T", t))
                    wait_drained(pe, ("v0", t))
                    for h in range(HP):
                        W = 2 * DK0
                        ins = nc.tensor.matmul(ps[:, h * 2 * W:h * 2 * W + 2 * W], probs_T[:, t % 2, h],
                                               v0[:, t % 2, :, h * W:h * W + W], start=True, stop=True)
                    end(key, ins)
                elif kind == "attended0_T":
                    wait_drained(pe, ("attended0", key[1]))
                    transposes(key, [att[:, key[1] % 2]])
                elif kind == "project0":
                    ps = begin(key)
                    wait_drained(pe, ("attended0_T", key[1]))
                    end(key, nc.tensor.matmul(ps[:, 0:D], att_T[:, key[1] % 2], wo0_T[:], start=True, stop=True))
                elif kind == "x1_T":
                    pe.wait_ge(sem("x1_ready"), 1)
                    transposes(key, [x1[:, key[1] * TH + j] for j in range(TH)])
                elif kind == "ffn0_up":
                    _, g, f = key
                    ps = begin(key)
                    wait_drained(pe, ("x1_T", g))
                    for j in range(2):
                        ins = nc.tensor.matmul(ps[:, j], w1_0T[:, (f + j) * P:(f + j + 1) * P],
                                               xn_T[:, g * TC:g * TC + TC], start=True, stop=True)
                    end(key, ins)
                elif kind == "ffn0_down":
                    g = key[1]
                    ps = begin(key)
                    wait_drained(pe, ("ffn0_up", g, FC - 2))
                    for j in range(TH):
                        for f in range(FC):
                            ins = nc.tensor.matmul(ps[:, j * D:j * D + D], hidden[:, g, f, j * P:j * P + P],
                                                   w2_0T[:, f], start=(f == 0), stop=(f == FC - 1))
                    end(key, ins)
                elif kind == "keys1":
                    ps = begin(key)
                    wait_drained(pe, ("qk_weight", 1))
                    for g in range(HALVES):
                        ins = nc.tensor.matmul(ps[:, g], qk_w[:, key[1]], ctx_T[:, g * TC:g * TC + TC],
                                               start=True, stop=True)
                    end(key, ins)
                elif kind == "gate":
                    ps = begin(key)
                    pe.wait_ge(sem("pooled"), 1)
                    for t in range(TILES):
                        ins = nc.tensor.matmul(ps[:, t * E:t * E + E], xn[:, t], gate_w_T[:], start=True, stop=True)
                    end(key, ins)
                elif kind == "experts":
                    t = key[1]
                    ps = begin(key)
                    wait_loaded(pe, "expert_b")
                    wait_drained(pe, ("xn_T", "experts"))
                    for j in range(2):
                        nc.tensor.matmul(ps[:, j], ones[0:1, :], expert_b[:, j * 512:j * 512 + 512],
                                         start=True, stop=False)
                        ins = nc.tensor.matmul(ps[:, j], xn_T[:, t * P:t * P + P],
                                               expert_w_T[:, 4 * j:4 * j + 4].rearrange("p e d -> p (e d)"),
                                               start=False, stop=True)
                    end(key, ins)
                elif kind == "values1":
                    _, t, b = key
                    ps = begin(key)
                    at = (2 * t + b) * KEYS
                    for j in range(2):
                        for h2 in range(2):
                            heads_j = vo_w[:].rearrange("p (h w) d -> p w h d", w=2)[:, h2, 4 * j:4 * j + 4]
                            ins = nc.tensor.matmul(ps[KEYS * h2:KEYS * h2 + KEYS, j], ctx_T[:, at:at + KEYS],
                                                   heads_j, start=True, stop=True)
                    end(key, ins)
                elif kind == "attended1":
                    t = key[1]
                    ps = begin(key)
                    wait_drained(pe, ("probs1_T", t))
                    wait_drained(pe, ("values1", t, 1))
                    for h in range(HP):
                        for b in range(2):
                            ins = nc.tensor.matmul(ps[S * b:S * b + S, 0:D], probs_T[:, t % 2, h, S * b:S * b + S],
                                                   values1[:, t % 2, b, h], start=(h == 0), stop=(h == HP - 1))
                    end(key, ins)
                elif kind == "router_T":
                    pe.wait_ge(sem("router_in"), 1)
                    transposes(key, [x1[:, t] for t in range(TILES)])
                elif kind == "router":
                    ps = begin(key)
                    wait_drained(pe, ("router_T",))
                    wait_loaded(pe, "ffn1")
                    for t in range(TILES):
                        ins = nc.tensor.matmul(ps[:, t * E:t * E + E], ctx_T[:, t * P:t * P + P], wr[:],
                                               start=True, stop=True)
                    end(key, ins)
                elif kind == "count":
                    ps = begin(key)
                    pe.wait_ge(sem("counted"), 2 * (key[1] + 1))
                    end(key, nc.tensor.matmul(ps[:, 0:2], groups[:], counted[:], start=True, stop=True))
                elif kind == "limits":
                    ps = begin(key)
                    pe.wait_ge(sem("picked"), 2)
                    end(key, nc.tensor.matmul(ps[:, 0:8], ones[:], picked[:].rearrange("p a b -> p (a b)"),
                                              start=True, stop=True))
                elif kind == "moe_up":
                    _, g, e, f = key
                    ps = begin(key)
                    wait_drained(pe, ("xn_T", "moe"))
                    if e == 1:
                        pe.wait_ge(sem("w1_perturbed"), 1)
                    w = (w1_1, w1_p)[e]
                    for j in range(2):
                        ins = nc.tensor.matmul(ps[:, j], w[:, (f + j) * P:(f + j + 1) * P],
                                               xn_T[:, g * TC:g * TC + TC], start=True, stop=True)
                    end(key, ins)
                elif kind == "moe_down":
                    _, g, e = key
                    ps = begin(key)
                    wait_drained(pe, ("moe_up", g, e, FC - 2))
                    if e == 1:
                        pe.wait_ge(sem("w2_perturbed"), 1)
                    w = (w2_1, w2_p)[e]
                    for j in range(TH):
                        for f in range(FC):
                            ins = nc.tensor.matmul(ps[:, j * D:j * D + D], hidden[:, e, f, j * P:j * P + P],
                                                   w[:, f], start=(f == 0), stop=(f == FC - 1))
                    end(key, ins)

            for key, _, _ in plan:
                run(key)


_INS = ['x', 'ctx_1024', 'fside_Bx1xSxS2_0', 'mask_Bx1xSxS2_bf0', 'L0_xattn_Wq', 'L0_xattn_Wo', 'L0_xattn_W1',
        'L0_xattn_b1', 'L0_xattn_W2', 'L0_xattn_b2', 'L0_xattn_g1', 'L0_xattn_be1', 'L0_xattn_g2', 'L0_xattn_be2',
        'L0_ffn_gate_w', 'L0_ffn_gate_b', 'L0_ffn_expert_w', 'L0_ffn_expert_b', 'L1_xattn_Wq', 'L1_xattn_Wk',
        'L1_xattn_Wv', 'L1_xattn_Wo', 'L1_ffn_W1', 'L1_ffn_b1', 'L1_ffn_W2', 'L1_ffn_b2', 'L1_ffn_ln_gamma',
        'L1_ffn_ln_beta', 'L1_ffn_Wr', 'L1_ffn_br']


def kernel(**inputs):
    import numpy as _np
    import concourse.bacc as _bacc
    from concourse import mybir as _mybir
    from concourse.bass_utils import run_bass_kernel_spmd as _run

    nc = _bacc.Bacc("TRN2", target_bir_lowering=False, num_devices=1)
    arrays, args = {}, {}
    for name in _INS:
        a = _np.ascontiguousarray(inputs[name])
        arrays[f"in_{name}_dram"] = a
        args[name] = nc.dram_tensor(f"in_{name}_dram", a.shape, _mybir.dt.from_np(a.dtype), kind="ExternalInput").ap()
    shape = inputs["x"].shape
    out = nc.dram_tensor("out_0_dram", shape, _mybir.dt.float32, kind="ExternalOutput").ap()
    build(nc, args, out)
    r = _run(nc, [arrays], core_ids=[0])
    return r.results[0]["out_0_dram"]
```

```python
from contextlib import ExitStack

import concourse.bass as bass
from concourse import mybir

ALU = mybir.AluOpType
ACT = mybir.ActivationFunctionType
AX = mybir.AxisListType.X
F32 = mybir.dt.float32
BF16 = mybir.dt.bfloat16
I32 = mybir.dt.int32
U8 = mybir.dt.uint8
U16 = mybir.dt.uint16

P = 128
TILES = 8
HALVES = 2
TH = TILES // HALVES
HEADS = 16
BITS = 31
HIGH_BITS = 15
EPS = 1e-5
FAR = -3.0e38


ORDER = """
    norm_stats:attn0,0 expand_mask norm:attn0,0 norm_stats:attn0,1 transpose_w0 norm:attn0,1 transpose_ctx
    transpose:attn0,0 decide:0 count:0 weight_T:wo1 project_q0:0 sign:0 combine:0 split_bias project_k0
    fold_weights:qk,0 expand_keys0:0 decide:1 sign:1 count:1 combine:1 fold_weights:qk,1 expand_keys0:1
    weight_T:experts decide:2 count:2 sign:2 weight_T:ffn0 scores0:0 expand_keys0:2 fold_weights:vo,0 combine:2
    scores0:1 transpose:attn0,1 fold_weights:vo,1 clear_values decide:3 count:3 project_q0:1 shift0:0 exp0:0 sign:3
    scores0:2 transpose_probs0:0 shift0:1 combine:3 expand_keys0:3 exp0:1 values0:0 values0:1 shift0:2
    transpose_probs0:1 decide:4 count:4 sign:4 expand_keys0:4 exp0:2 scores0:3 shift0:3 attend0:0
    transpose_probs0:2 combine:4 attend0:1 exp0:3 decide:5 count:5 sign:5 scores0:4 transpose_probs0:3
    expand_keys0:5 attend0:2 combine:5 attend0:3 expand_keys0:6 keys1:0 decide:6 count:6 transpose_att:0 values0:2
    project0:0 sign:6 combine:6 shift0:4 exp0:4 norm_stats:x1,0 keys1:1 decide:7 norm:x1,0 transpose_probs0:4
    scores0:5 scores0:6 transpose:x1,0 bias_x1:0 values0:3 sign:7 expand_keys0:7 count:7 combine:7 up0:0,0 up0:0,2
    scores0:7 shift0:5 down0:0 decide:8 shift0:6 shift0:7 exp0:5 exp0:6 norm_stats:ffn0,0 count:8 sign:8
    transpose_probs0:5 exp0:7 combine:8 norm:ffn0,0 keys1:2 keys1:3 decide:9 norm_stats:experts,0 count:9
    norm:experts,0 keys1:4 attend0:4 attend0:5 sign:9 transpose_probs0:6 keys1:5 combine:9 decide:10 count:10
    transpose:experts,0 pool_gate:0 sign:10 combine:10 transpose_probs0:7 experts:0 decide:11 sign:11 count:11
    gate:0 attend0:6 attend0:7 exp_gate:0 experts:1 combine:11 weigh_gate:0 weigh_experts:0 weigh_experts:1
    decide:12 count:12 transpose_att:1 add_experts:0 sign:12 combine:12 experts:2 keys1:6 add_experts:1 decide:13
    project0:1 norm_stats:x1,1 count:13 sign:13 keys1:7 combine:13 experts:3 weigh_experts:2 weigh_experts:3
    norm:x1,1 keys1:8 decide:14 sign:14 add_experts:2 add_experts:3 norm_stats:attn1,0 keys1:9 count:14
    transpose:x1,1 bias_x1:1 keys1:10 combine:14 up0:1,0 up0:1,2 norm:attn1,0 decide:15 keys1:11 down0:1
    norm_stats:ffn0,1 transpose:attn1,0 count:15 sign:15 combine:15 norm:ffn0,1 keys1:12 keys1:13 keys1:14
    decide:16 sign:16 norm_stats:experts,1 count:16 combine:16 keys1:15 norm:experts,1 values1:0 decide:17 count:17
    scores1:0 shift1:0 transpose:experts,1 scores1:1 shift1:1 sign:17 pool_gate:1 exp1:0 combine:17 values1:1
    exp1:1 sums1:0 decide:18 gate:1 sign:18 count:18 combine:18 exp_gate:1 experts:4 sums1:1 decide:19 count:19
    sign:19 combine:19 scale1:0 transpose_probs1:0 scale1:1 weigh_gate:1 weigh_experts:4 experts:5 weigh_experts:5
    decide:20 sign:20 count:20 combine:20 transpose_probs1:1 experts:6 weigh_experts:6 add_experts:4 decide:21
    sign:21 add_experts:5 attend1:0 count:21 combine:21 experts:7 add_experts:6 weigh_experts:7 decide:22 count:22
    attend1:1 add_experts:7 sign:22 combine:22 scores1:2 decide:23 count:23 sign:23 combine:23 values1:2
    norm_stats:attn1,1 decide:24 sign:24 count:24 combine:24 values1:3 norm:attn1,1 decide:25 sign:25 count:25
    combine:25 scores1:3 shift1:2 exp1:2 transpose:attn1,1 decide:26 sign:26 count:26 combine:26 shift1:3 exp1:3
    sums1:2 decide:27 sums1:3 sign:27 count:27 combine:27 scores1:4 scale1:2 transpose_probs1:2 scale1:3
    transpose_probs1:3 decide:28 count:28 attend1:2 sign:28 combine:28 decide:29 sign:29 count:29 combine:29
    attend1:3 decide:30 shift1:4 exp1:4 count:30 sign:30 combine:30 decide:31 limits values1:4 perturb:b1 sums1:4
    scale1:4 transpose_probs1:4 values1:5 perturb:w1 perturb:w2 perturb:b2 norm_stats:moe,0 norm:moe,0 attend1:4
    norm_stats:router,0 norm:router,0 values1:6 transpose:moe,0 scores1:5 up1:0,0,0 up1:0,0,2 transpose:router,0
    scores1:6 shift1:5 exp1:5 sums1:5 scale1:5 router:0 exp_router:0 weigh_router:0 scores1:7 down1:0,0
    transpose_probs1:5 shift1:6 shift1:7 exp1:6 exp1:7 sums1:6 scale1:6 up1:0,1,0 attend1:5 values1:7
    transpose_probs1:6 up1:0,1,2 sums1:7 scale1:7 transpose_probs1:7 attend1:6 attend1:7 norm_stats:moe,1
    norm:moe,1 norm_stats:router,1 down1:0,1 transpose:moe,1 up1:1,0,0 up1:1,0,2 norm:router,1 up1:1,1,0
    transpose:router,1 up1:1,1,2 router:1 exp_router:1 weigh_router:1 down1:1,0 down1:1,1
"""


def schedule():
    todo = []
    for word in ORDER.split():
        step, _, n = word.partition(":")
        todo.append((step, tuple(int(i) if i.isdigit() else i for i in n.split(",")) if n else ()))
    return todo


def products(item):
    step, n = item
    return {
        "transpose_w0": [("small", "act")],
        "transpose_ctx": [("big", "act")],
        "project_k0": [("big", "act")],
        "project_q0": [("small", "act")],
        "weight_T": [("big", "act")],
        "fold_weights": [("big", "act")],
        "values0": [("small", "dve")],
        "scores0": [("big", "dve")],
        "transpose_probs0": [("big", "act")],
        "attend0": [("small", "dve")],
        "transpose_att": [("small", "act")],
        "project0": [("small", "dve")],
        "transpose": [("small", "act")],
        "up0": [("big", "act")],
        "down0": [("small", "dve")],
        "gate": [("small", "dve")],
        "experts": [("big", "act")],
        "keys1": [("big", "act")],
        "values1": [("big", "act")] * 2,
        "scores1": [("big", "dve")],
        "transpose_probs1": [("big", "act")],
        "attend1": [("small", "dve")],
        "router": [("small", "dve")],
        "up1": [("big", "act")],
        "down1": [("small", "dve")],
        "decide": [("small", "dve")] if step == "decide" and n[0] >= 1 else [],
        "limits": [("small", "dve")],
    }.get(step, [])


class Rings:

    SLOTS = {"big": 3, "small": 2}

    def __init__(self, todo):
        self.slot, self.filled, self.drained, self.before = {}, {}, {}, {}
        order = {"big": [], "small": []}
        drains = {"act": 0, "dve": 0}
        for item in todo:
            for j, (ring, drain) in enumerate(products(item)):
                key, n = (*item, j), len(order[ring])
                self.slot[key] = (ring, n % self.SLOTS[ring])
                self.filled[key] = (ring, n + 1)
                self.before[key] = order[ring][n - self.SLOTS[ring]] if n >= self.SLOTS[ring] else None
                order[ring].append(key)
                drains[drain] += 1
                self.drained[key] = (drain, drains[drain])


class Buffers:

    def __init__(self, todo, steps, count):
        users = [item for item in todo if item[0] in steps]
        self.at = {item: n % count for n, item in enumerate(users)}
        self.before = {item: users[n - count] if n >= count else None for n, item in enumerate(users)}


def build(nc, a, out):
    B, S, D = a["x"].shape
    TOK = B * S
    TC = TH * P
    H, HP = HEADS, HEADS // 2
    DK0 = D // H
    DK1 = a["L1_xattn_Wq"].shape[0] // H
    E = a["L0_ffn_gate_w"].shape[0]
    F = a["L0_xattn_W1"].shape[0]
    FC = F // P
    KEYS = a["ctx_1024"].shape[1]
    VW = 2 * DK0 + 2
    SCALE0 = 1.0 / float(D) ** 0.5
    SPARSITY, GAIN = 0.1, 0.8
    sizes = [F * D, F * D, F, D]
    low = [max(1, int(n * SPARSITY / 2)) for n in sizes]
    high = [n - k + 1 for n, k in zip(sizes, low)]
    GROUP = P // 4
    RW, RB = F * D // GROUP, F // GROUP
    BY_DVE = RW * 3 // 8
    assert TOK == TILES * P and S == 64 and KEYS == 64 and D == P and DK1 == 64 and F == 4 * P and E == 8

    todo = schedule()
    rings = Rings(todo)
    norms = [n for step, n in todo if step == "norm"]
    norm_stats = [n for step, n in todo if step == "norm_stats"]
    work_ring = Buffers(todo, ("scores0", "scores1", "experts"), 3)
    probs_ring = Buffers(todo, ("transpose_probs0", "transpose_probs1"), 2)
    wide_ring = Buffers(todo, ("expand_keys0", "values1"), 2)
    v0_ring = Buffers(todo, ("values0",), 2)

    with ExitStack() as ctx:
        def sb(name, shape, dt=F32):
            return ctx.enter_context(nc.sbuf_tensor(name, shape, dt))

        named = {}

        def sem(name):
            if name not in named:
                named[name] = ctx.enter_context(nc.semaphore(name))
            return named[name]

        xt = sb("xt", [P, TILES, D])
        ctx_tok = sb("ctx_tok", [P, TILES, D])
        fside = sb("fside", [P, TILES, KEYS])
        mask_in = sb("mask_in", [P, TILES, KEYS], U8)
        mask_add = sb("mask_add", [P, TILES, KEYS])
        wq0 = sb("wq0", [P, D])
        wo0 = sb("wo0", [P, D])
        w1_0 = sb("w1_0", [P, FC, D])
        w2_0 = sb("w2_0", [P, F])
        b1_rows = sb("b1_rows", [2 * FC, P])
        b1_cols = sb("b1_cols", [P, 2 * FC])
        b1_0, b1_1 = b1_cols[:, 0:FC], b1_cols[:, FC:2 * FC]
        rows = {n: sb(n, [P, D]) for n in ("row_b2", "row_g1", "row_be1", "row_g2", "row_be2", "row_gamma",
                                           "row_beta", "row_y0", "row_y1")}
        gate_w = sb("gate_w", [E, D])
        row_gate_b = sb("row_gate_b", [P, E])
        row_br = sb("row_br", [P, E])
        expert_w = sb("expert_w", [P, E, D])
        expert_b = sb("expert_b", [E, D])
        expert_b_part = sb("expert_b_part", [E, 3, D], BF16)
        expert_b_rows = sb("expert_b_rows", [3, E * D], BF16)
        ones_bf = sb("ones_bf", [3, P], BF16)
        raw1 = sb("raw1", [P, 4, HP, D])
        wq1, wk1, wv1, wo1 = (raw1[:, i] for i in range(4))
        w1_1 = sb("w1_1", [P, F])
        w2_1 = sb("w2_1", [P, FC, D])
        wr = sb("wr", [P, E])
        ranked_w = sb("ranked_w", [P, RW])
        ranked_b = sb("ranked_b", [P, RB])
        below = sb("below", [P, RW], BF16)
        below_b = sb("below_b", [P, RB], BF16)

        ident = sb("ident", [P, P])
        ones = sb("ones", [P, P])
        groups = sb("groups", [P, P])
        head_mask = sb("head_mask", [P, H])
        pair_mask = sb("pair_mask", [P, 2, DK0])
        half_exp = sb("half_exp", [P, TH])

        wq0_T = sb("wq0_T", [P, D])
        wo0_T = sb("wo0_T", [P, D])
        gate_w_T = sb("gate_w_T", [P, E])
        w1_0T = sb("w1_0T", [P, F])
        w2_0T = sb("w2_0T", [P, FC, D])
        expert_w_T = sb("expert_w_T", [P, E, D])
        qk_w = sb("qk_w", [P, H, D])
        vo_w = sb("vo_w", [P, H, D])
        w1_p = w1_0[:].rearrange("p c d -> p (c d)")
        w2_p = w2_0[:].rearrange("p (c d) -> p c d", c=FC)
        b1_p = sb("b1_p", [P, FC])

        xn = sb("xn", [P, TILES, D])
        xn_T = sb("xn_T", [P, TOK])
        ctx_T = sb("ctx_T", [P, TOK])
        keys1 = sb("keys1", [P, H, TOK])
        q0_T, k0_T = keys1[:, H - 1], keys1[:, H - 2]
        wide = sb("wide", [P, 2, 2 * H * KEYS])
        work = sb("work", [P, 3, H, KEYS])
        probs_T = sb("probs_T", [P, 2, HP, P])
        att_T = sb("att_T", [P, TC])
        raw1_flat = raw1[:].rearrange("p a h d -> p (a h d)")
        hidden = raw1_flat.rearrange("p (e f t) -> p e f t", e=2, f=FC)
        V0, ATT = 2 * 4 * HP * VW, 2 * HP * D
        v0 = raw1_flat[:, ATT:ATT + V0].rearrange("p (n b c v) -> p n b c v", n=2, b=4, c=HP)
        att = raw1_flat[:, ATT + V0:ATT + V0 + TH * D].rearrange("p (t d) -> p t d", t=TH)
        row_max = sb("row_max", [P, TILES, H])
        row_sum = row_max
        row_inv = sb("row_inv", [P, TILES, H])
        stats = sb("stats", [P, TILES, 6])
        moments = sb("moments", [P, TILES, 2])
        var_eps = sb("var_eps", [P, TILES])
        rstd = sb("rstd", [P, TILES])
        res = ctx_tok
        wo1_T = res
        x1 = expert_w
        pooled_T = sb("pooled_T", [P, B])
        logits = sb("logits", [P, TILES, E])
        best = sb("best", [P, TILES, 8])
        weights = sb("weights", [P, TILES, E])
        kept = sb("kept", [P, TILES, E])
        total = sb("total", [P, TILES])
        gates = sb("gates", [P, TILES, E])
        expert_sum = sb("expert_sum", [P, D])
        expert_b_rest = expert_sum[0:E]
        share = sb("share", [P, TILES, 2])
        limit = sb("limit", [P, 2])
        tried = sb("tried", [P, 2])
        high_part = sb("high_part", [P, 2])
        counted = sb("counted", [P, 2])
        signs = sb("signs", [P, 1])
        rank = sb("rank", [P, 2])
        keep_bit = sb("keep_bit", [P, 2])
        base = sb("base", [P, 2])
        limit_bits = sb("limit_bits", [P, 2, 2], I32)
        picks = sb("picks", [P, 4])
        picked = sb("picked", [P, 2, 4])
        limits = sb("limits", [P, 2, 4])
        size, tier, tier2 = (ranked_w[:, h * F:h * F + F] for h in range(3))

        big = [ctx.enter_context(nc.psum_tensor(f"big{i}", [P, 2, 512], F32)) for i in range(Rings.SLOTS["big"])]
        small = [ctx.enter_context(nc.psum_tensor(f"small{i}", [P, 512], F32)) for i in range(Rings.SLOTS["small"])]

        def psum(key):
            ring, n = rings.slot[key]
            return big[n] if ring == "big" else small[n]

        def wait_filled(eng, step, n=(), j=0):
            ring, count = rings.filled[(step, n, j)]
            eng.wait_ge(sem(f"{ring}_filled"), count)

        def wait_drained(eng, step, n=(), j=0):
            who, count = rings.drained[(step, n, j)]
            eng.wait_ge(sem(f"{who}_drained"), count)

        def wait_norm(eng, name, g):
            eng.wait_ge(sem("norm_done"), norms.index((name, g)) + 1)

        def wait_work_free(eng, item):
            before = work_ring.before[item]
            if before is not None and before[0] == "experts":
                eng.wait_ge(sem("experts_summed"), before[1][0] + 1)
            elif before is not None:
                wait_filled(eng, f"transpose_probs{before[0][-1]}", before[1])

        def wait_wide_free(eng, item):
            before = wide_ring.before[item]
            if before is not None:
                wait_filled(eng, "scores0" if before[0] == "expand_keys0" else "attend1", before[1])

        def work_of(step, t):
            return work[:, work_ring.at[(step, (t,))]]

        def probs_of(layer, t):
            return probs_T[:, probs_ring.at[(f"transpose_probs{layer}", (t,))]]

        for name in ("big_filled", "small_filled", "act_drained", "dve_drained"):
            sem(name)

        tok = lambda ap: ap.rearrange("(t b) s d -> (b s) t d", b=2)
        half_tiles = lambda g: slice(g * TH, g * TH + TH)
        LOADS = [
            ("ctx", ctx_tok[:], tok(a["ctx_1024"])),
            ("w0", wq0[:], a["L0_xattn_Wq"]),
            ("x", xt[:], tok(a["x"])),
            ("w0", wo0[:], a["L0_xattn_Wo"]),
            ("w0", gate_w[:], a["L0_ffn_gate_w"]),
            ("w0", b1_rows[0:FC], a["L0_xattn_b1"].rearrange("(c p) -> c p", p=P)),
            ("w0", b1_rows[FC:2 * FC], a["L1_ffn_b1"].rearrange("(c p) -> c p", p=P)),
            ("mask", mask_in[:], a["mask_Bx1xSxS2_bf0"].rearrange("(t b) o s k -> (b o s) t k", b=2)),
            ("w1_qk", wo1[:].rearrange("p h d -> p (h d)"), a["L1_xattn_Wo"]),
            ("w1_qk", wq1[:], a["L1_xattn_Wq"].rearrange("(h p) d -> p h d", p=P)),
            ("w1_qk", wk1[:], a["L1_xattn_Wk"].rearrange("(h p) d -> p h d", p=P)),
            ("ranked", ranked_w[0:32], a["L1_ffn_W1"].rearrange("(p r) f -> p (r f)", p=GROUP)),
            ("ranked", ranked_w[32:64], a["L1_ffn_W1"].rearrange("(p r) f -> p (r f)", p=GROUP)),
            ("ranked", ranked_w[64:96], a["L1_ffn_W2"].rearrange("(p r) f -> p (r f)", p=GROUP)),
            ("ranked", ranked_w[96:128], a["L1_ffn_W2"].rearrange("(p r) f -> p (r f)", p=GROUP)),
            ("ranked", ranked_b[0:32], a["L1_ffn_b1"].rearrange("(p r) -> p r", p=GROUP)),
            ("ranked", ranked_b[32:64], a["L1_ffn_b1"].rearrange("(p r) -> p r", p=GROUP)),
            ("ranked_b2", ranked_b[64:96, 0:D // 32], a["L1_ffn_b2"].rearrange("(p r) -> p r", p=GROUP)),
            ("ranked_b2", ranked_b[96:128, 0:D // 32], a["L1_ffn_b2"].rearrange("(p r) -> p r", p=GROUP)),
            ("expert_b", expert_b[:], a["L0_ffn_expert_b"]),
            ("ffn0_w", w1_0[:], a["L0_xattn_W1"].rearrange("(c p) d -> p c d", p=P)),
            ("ffn0_w", w2_0[:], a["L0_xattn_W2"]),
            ("expert_w", expert_w[:], a["L0_ffn_expert_w"].rearrange("e o d -> o e d")),
            ("w1_v", wv1[:], a["L1_xattn_Wv"].rearrange("(h p) d -> p h d", p=P)),
        ] + [("rows", t[:], a[n].partition_broadcast(P)) for t, n in (
            (rows["row_g1"], "L0_xattn_g1"), (rows["row_be1"], "L0_xattn_be1"), (rows["row_b2"], "L0_xattn_b2"),
            (rows["row_g2"], "L0_xattn_g2"), (rows["row_be2"], "L0_xattn_be2"), (rows["row_gamma"], "L1_ffn_ln_gamma"),
            (rows["row_beta"], "L1_ffn_ln_beta"), (rows["row_y0"], "L1_ffn_b2"), (row_gate_b, "L0_ffn_gate_b"),
            (row_br, "L1_ffn_br"))] + [
            ("fside", fside[:], a["fside_Bx1xSxS2_0"].rearrange("(t b) o s k -> (b o s) t k", b=2)),
            ("ffn1", w1_1[:], a["L1_ffn_W1"]),
            ("ffn1", w2_1[:], a["L1_ffn_W2"].rearrange("(c p) d -> p c d", p=P)),
            ("ffn1", wr[:], a["L1_ffn_Wr"]),
        ]
        loaded = {}
        for name, _, _ in LOADS:
            loaded[name] = loaded.get(name, 0) + 16
            sem(f"loaded_{name}")

        def wait_loaded(eng, name):
            eng.wait_ge(sem(f"loaded_{name}"), loaded[name])

        def searched(ranked, r):
            if r < HIGH_BITS:
                return ranked[:].bitcast(U16).rearrange("p (n two) -> p n two", two=2)[:, :, 1]
            return ranked[:]

        block = ctx.enter_context(nc.Block())

        @block.sync
        def _(sp):
            for name, dst, src in LOADS:
                if name == "ranked_b2":
                    sp.wait_ge(sem("bias_padded"), 1)
                sp.dma_start(dst, src).then_inc(sem(f"loaded_{name}"), 16)
            sp.wait_ge(sem("bias_split"), 1)
            for j in range(3):
                sp.dma_start(expert_b_rows[j:j + 1], expert_b_part[:, j]).then_inc(sem("bias_rows"), 16)
            out_tok = tok(out)
            for g in range(HALVES):
                sp.wait_ge(sem("x_done"), TH * (g + 1))
                sp.dma_start(out_tok[:, half_tiles(g)], xt[:, half_tiles(g)]).then_inc(sem("stored"), 16)
            sp.wait_ge(sem("stored"), 16 * HALVES)

        @block.gpsimd
        def _(pool):
            nc.gpsimd.memset(ident[:], 0.0).then_inc(sem("pool_step"), 1)
            nc.gpsimd.memset(head_mask[:], 1.0).then_inc(sem("pool_step"), 1)
            nc.gpsimd.memset(half_exp[:], -0.5).then_inc(sem("pool_step"), 1)
            pool.wait_ge(sem("pool_step"), 3)
            nc.gpsimd.affine_select(out=ident[:], in_=ident[:], compare_op=ALU.not_equal, fill=1.0, base=0,
                                    pattern=[[-1, P]], channel_multiplier=1).then_inc(sem("ident_ready"), 1)
            nc.gpsimd.affine_select(out=head_mask[:], in_=head_mask[:], compare_op=ALU.is_ge, fill=0.0, base=0,
                                    pattern=[[-DK0, H]], channel_multiplier=1).then_inc(sem("pool_step"), 1)
            pool.wait_ge(sem("pool_step"), 4)
            nc.gpsimd.affine_select(out=head_mask[:], in_=head_mask[:], compare_op=ALU.is_ge, fill=0.0, base=DK0 - 1,
                                    pattern=[[DK0, H]], channel_multiplier=-1).then_inc(sem("pool_step"), 1)
            pool.wait_ge(sem("pool_step"), 5)

            def by_head(ap):
                return ap.unsqueeze(2).broadcast_to([P, H, KEYS])

            for step, n in todo:
                if step == "norm_stats":
                    tiles, k = half_tiles(n[1]), norm_stats.index(n)
                    pool.wait_ge(sem("var_ready"), k + 1)
                    nc.gpsimd.tensor_tensor(rstd[:, tiles], var_eps[:, tiles], half_exp[:],
                                            ALU.pow).then_inc(sem("rstd_ready"), 1)
                elif step == "expand_keys0":
                    t = n[0]
                    wait_drained(pool, "project_k0")
                    wait_wide_free(pool, (step, n))
                    dst = wide[:, wide_ring.at[(step, n)]].rearrange("p (h k) -> p h k", h=H)
                    nc.gpsimd.tensor_tensor(dst, k0_T[:, t * P:t * P + P].unsqueeze(1).broadcast_to([P, H, P]),
                                            head_mask[:].unsqueeze(2).broadcast_to([P, H, P]),
                                            ALU.mult).then_inc(sem("keys0_expanded"), 1)
                elif step in ("shift0", "shift1"):
                    t, buf = n[0], work_of("scores" + step[-1], n[0])
                    pool.wait_ge(sem(f"max{step[-1]}_ready"), t + 1)
                    nc.gpsimd.tensor_tensor(buf, buf, by_head(row_max[:, t]),
                                            ALU.subtract).then_inc(sem(f"shifted{step[-1]}"), 1)
                elif step == "weigh_experts":
                    t = n[0]
                    wait_drained(pool, "experts", n)
                    pool.wait_ge(sem("gates_ready"), t // TH + 1)
                    buf = work_of("experts", t).rearrange("p h k -> p (h k)").rearrange("p (e d) -> p e d", e=E)
                    nc.gpsimd.tensor_tensor(buf, buf, gates[:, t].unsqueeze(2).broadcast_to([P, E, D]),
                                            ALU.mult).then_inc(sem("experts_weighed"), 1)
                elif step == "scale1":
                    t, buf = n[0], work_of("scores1", n[0])
                    pool.wait_ge(sem("inverse1"), t + 1)
                    nc.gpsimd.tensor_tensor(buf, buf, by_head(row_inv[:, t]), ALU.mult).then_inc(sem("probs1"), 1)

        @block.scalar
        def _(act):
            def drain(dst, key, src=None, func=ACT.Copy, last=True, **kw):
                wait_filled(act, *key)
                ins = nc.scalar.activation(dst, psum(key)[:] if src is None else src, func, **kw)
                if last:
                    ins.then_inc(sem("act_drained"), 1)

            def two(ap):
                return ap.rearrange("p (a n) -> p a n", a=2)

            def exponentials(layer, t, buf):
                act.wait_ge(sem(f"shifted{layer}"), t + 1)
                nc.scalar.activation(buf, buf, ACT.Exp).then_inc(sem(f"exp{layer}"), 1)

            for step, n in todo:
                key = (step, n, 0)
                if step == "transpose_w0":
                    ps = psum(key)
                    drain(wq0_T[:], key, ps[:, 0:D], last=False)
                    drain(wo0_T[:], key, ps[:, D:2 * D], last=False)
                    drain(gate_w_T[:], key, ps[:, 2 * D:2 * D + E], last=False)
                    drain(b1_cols[:], key, ps[:, 3 * D:3 * D + 2 * FC])
                elif step == "transpose_ctx":
                    drain(two(ctx_T[:]), key)
                elif step == "project_k0":
                    drain(two(k0_T), key)
                elif step == "project_q0":
                    drain(q0_T[:, n[0] * TC:n[0] * TC + TC], key)
                elif step == "transpose":
                    dst = ctx_T if n[0] == "router" else xn_T
                    drain(dst[:, n[1] * TC:n[1] * TC + TC], key)
                elif step == "weight_T":
                    if n[0] == "ffn0":
                        drain(w1_0T[:], key, psum(key)[:, 0], last=False)
                        drain(w2_0T[:].rearrange("p c d -> p (c d)"), key, psum(key)[:, 1])
                    else:
                        dst = expert_w_T if n[0] == "experts" else wo1_T
                        drain(two(dst[:].rearrange("p e d -> p (e d)")), key)
                elif step == "fold_weights":
                    dst = (qk_w if n[0] == "qk" else vo_w)[:, n[1] * HP:n[1] * HP + HP]
                    drain(dst.rearrange("p (h w) d -> p w h d", w=2), key,
                          psum(key)[:].rearrange("p w (h d) -> p w h d", d=D))
                elif step in ("exp0", "exp1"):
                    exponentials(int(step[-1]), n[0], work_of("scores" + step[-1], n[0]))
                elif step in ("transpose_probs0", "transpose_probs1"):
                    layer, before = int(step[-1]), probs_ring.before[(step, n)]
                    if before is not None:
                        wait_filled(act, f"attend{before[0][-1]}", before[1])
                    drain(two(probs_of(layer, n[0]).rearrange("p h q -> p (h q)")), key)
                elif step == "transpose_att":
                    drain(att_T[:], key)
                elif step == "up0":
                    g, f = n
                    wait_drained(act, "fold_weights", ("vo", 1))
                    for j in range(2):
                        drain(hidden[:, g, f + j], key, psum(key)[:, j], ACT.Gelu, last=(j == 1),
                              bias=b1_0[:, f + j:f + j + 1])
                elif step == "keys1":
                    drain(two(keys1[:, n[0]]), key)
                elif step == "exp_gate":
                    act.wait_ge(sem("gate_shifted"), n[0] + 1)
                    w = weights[:, half_tiles(n[0])]
                    nc.scalar.activation(w, w, ACT.Exp).then_inc(sem("gate_exp"), 1)
                elif step == "experts":
                    wait_work_free(act, (step, n))
                    drain(two(work_of(step, n[0]).rearrange("p h k -> p (h k)")), key, func=ACT.Gelu)
                elif step == "values1":
                    wait_wide_free(act, (step, n))
                    for b in range(2):
                        dst = wide[:, wide_ring.at[(step, n)], b * HP * D:(b + 1) * HP * D]
                        drain(two(dst), (step, n, b))
                elif step == "exp_router":
                    act.wait_ge(sem("router_shifted"), n[0] + 1)
                    w = weights[:, half_tiles(n[0])]
                    nc.scalar.activation(w, w, ACT.Exp).then_inc(sem("router_exp"), 1)
                elif step == "up1":
                    g, e, f = n
                    if e == 1:
                        act.wait_ge(sem("b1_perturbed"), 1)
                    if g == 1:
                        wait_filled(act, "down1", (0, e))
                    for j in range(2):
                        drain(hidden[:, e, f + j], key, psum(key)[:, j], ACT.Gelu_apprx_tanh, last=(j == 1),
                              bias=(b1_1 if e == 0 else b1_p)[:, f + j:f + j + 1])
                elif step == "sign":
                    r = n[0]
                    act.wait_ge(sem("tried"), r + 1)
                    if r >= 1:
                        act.wait_ge(sem("combined"), r)
                    keys = searched(ranked_w, r)[:, BY_DVE:RW]
                    nc.scalar.activation(below[:, BY_DVE:RW], keys, ACT.Sign, bias=tried[:, 0:1], scale=-1.0,
                                         accum_out=signs[:, 0:1]).then_inc(sem("signs_ready"), 1)

        @block.vector
        def _(dve):
            V = nc.vector
            steps = [0]

            def step_done(ins):
                steps[0] += 1
                ins.then_inc(sem("dve_step"), 1)
                return steps[0]

            def after(n):
                dve.wait_ge(sem("dve_step"), n)

            def drained(ins):
                ins.then_inc(sem("dve_drained"), 1)

            def across(row, tiles=TH):
                return row[:].unsqueeze(1).broadcast_to([P, tiles, row.shape[-1]])

            def wide8(ap):
                return ap.broadcast_to([P, TH, E])

            def constants():
                V.memset(ones[:], 1.0).then_inc(sem("ones_ready"), 1)
                V.memset(ranked_b[64:128], 3.0e38).then_inc(sem("bias_padded"), 1)
                step_done(V.memset(ones_bf[:], 1.0))
                step_done(V.memset(groups[:], 0.0))
                step_done(V.memset(pair_mask[:], 0.0))
                step_done(V.memset(mask_add[:], 0.0))
                step_done(V.memset(work[:, 0], FAR))
                m = step_done(V.memset(picks[:], 0.0))
                for g in range(4):
                    ranks = [low, high][g % 2]
                    step_done(V.memset(rank[32 * g:32 * g + 32, 0:1],
                                       float(ranks[g // 2] - 1) - 0.5 * GROUP * (RW - BY_DVE)))
                    step_done(V.memset(rank[32 * g:32 * g + 32, 1:2], float(ranks[2 + g // 2] - 1)))
                after(m)
                for g in range(4):
                    own = slice(32 * g, 32 * g + 32)
                    step_done(V.memset(groups[own, own], 1.0))
                    step_done(V.memset(picks[32 * g:32 * g + 1, g:g + 1], 1.0))
                for h2 in range(2):
                    rows_h = slice(64 * h2, 64 * h2 + 64)
                    m = step_done(V.memset(pair_mask[rows_h, h2], 1.0))
                return m

            def ones_beside_values():
                wait_filled(dve, "fold_weights", ("vo", 1))
                after(step_done(V.memset(v0, 0.0)))
                for h2 in range(2):
                    for i in range(2):
                        at = 2 * DK0 + h2
                        m = step_done(V.memset(v0[64 * h2:64 * h2 + 64, i, :, :, at:at + 1], 1.0))
                after(m)

            def norm_source(name):
                return {"x1": res, "ffn0": res, "router": xn}.get(name, xt)

            def norm_stats_(n):
                name, g = n
                tiles, half, src = range(g * TH, g * TH + TH), half_tiles(g), norm_source(name)
                if name == "attn0":
                    wait_loaded(dve, "x")
                for t in tiles:
                    m = step_done(V.bn_stats(stats[:, t], src[:, t]))
                after(m)
                for t in tiles:
                    m = step_done(V.bn_aggr(moments[:, t], stats[:, t]))
                after(m)
                V.tensor_scalar(var_eps[:, half], moments[:, half, 1], EPS, None, ALU.add)\
                 .then_inc(sem("var_ready"), 1)

            def norm(n):
                name, g = n
                tiles, half, src = range(g * TH, g * TH + TH), half_tiles(g), norm_source(name)
                gain, shift = {"x1": ("row_g1", "row_be1"), "ffn0": ("row_g2", "row_be2"),
                               "router": ("row_gamma", "row_beta")}.get(name, (None, None))
                dst = xn if gain is None else x1
                if name == "x1":
                    wait_filled(dve, "weight_T", ("experts",))
                dve.wait_ge(sem("rstd_ready"), norm_stats.index(n) + 1)
                for t in tiles:
                    ins = V.tensor_scalar(dst[:, t], src[:, t], moments[:, t, 0:1], rstd[:, t:t + 1],
                                          ALU.subtract, ALU.mult)
                    if gain is None and t == tiles[-1]:
                        ins.then_inc(sem("norm_done"), 1)
                    else:
                        m = step_done(ins)
                if gain is not None:
                    after(m)
                    wait_loaded(dve, "rows")
                    m = step_done(V.tensor_tensor(dst[:, half], dst[:, half], across(rows[gain]), ALU.mult))
                    after(m)
                    V.tensor_tensor(dst[:, half], dst[:, half], across(rows[shift]), ALU.add)\
                     .then_inc(sem("norm_done"), 1)
                wait_norm(dve, name, g)
                after(m)
                if name == "ffn0":
                    after(step_done(V.tensor_tensor(xt[:, half], xt[:, half], x1[:, half], ALU.add)))

            def scores(layer, n):
                t, item = n[0], (f"scores{layer}", n)
                key = (*item, 0)
                wait_filled(dve, *key)
                wait_work_free(dve, item)
                added = (mask_add if layer == 0 else fside)[:, t].unsqueeze(1).broadcast_to([P, H, KEYS])
                buf = work_of(*item[:1], t)
                drained(V.scalar_tensor_tensor(out=buf, in0=psum(key)[:].rearrange("p a (h k) -> p (a h) k", k=KEYS),
                                               scalar=SCALE0 if layer == 0 else 1.0, in1=added,
                                               op0=ALU.mult, op1=ALU.add))
                wait_drained(dve, *key)
                V.tensor_reduce(row_max[:, t], buf, AX, ALU.max).then_inc(sem(f"max{layer}_ready"), 1)

            def attend0(n):
                t, key = n[0], ("attend0", n, 0)
                wait_filled(dve, *key)
                if t >= TH:
                    wait_filled(dve, "transpose_att", (0,))
                src = psum(key)[:, 0:HP * 2 * VW].rearrange("p (c b v) -> p c b v", b=2, v=VW)
                after(step_done(V.reciprocal(row_inv[:, t].rearrange("p (c w) -> p c w", w=2),
                                             src[:, :, 0, 2 * DK0:VW])))
                for b in range(2):
                    rows_b = slice(S * b, S * b + S)
                    inv = row_inv[rows_b, t].rearrange("p (c w) -> p c w", w=2).unsqueeze(3)
                    ins = V.tensor_tensor(att[rows_b, t % TH].rearrange("p (c w d) -> p c w d", w=2, d=DK0),
                                          src[rows_b, :, b, 0:2 * DK0].rearrange("p c (w d) -> p c w d", w=2),
                                          inv.broadcast_to([S, HP, 2, DK0]), ALU.mult)
                    if b == 1:
                        drained(ins)
                    else:
                        step_done(ins)

            def magnitudes():
                wait_loaded(dve, "ranked")
                wait_loaded(dve, "ranked_b2")
                for ranked in (ranked_w, ranked_b):
                    m = step_done(V.tensor_scalar(ranked[:].bitcast(I32), ranked[:].bitcast(I32), 0x7FFFFFFF, None,
                                                  ALU.bitwise_and))
                after(m)

            def bit_of(r):
                top = HIGH_BITS if r < HIGH_BITS else BITS
                return float(1 << (top - 1 - r))

            def keep_or_not(r, key, dst):
                wait_filled(dve, *key)
                drained(V.tensor_tensor(keep_bit[:], psum(key)[:, 0:2], rank[:], ALU.is_le))
                wait_drained(dve, *key)
                dve.wait_ge(sem("based"), r + 1)
                return V.scalar_tensor_tensor(out=dst, in0=keep_bit[:], scalar=bit_of(r), in1=base[:],
                                              op0=ALU.mult, op1=ALU.add)

            def low_keys():
                for j, (ranked, mark) in enumerate(((ranked_w, below), (ranked_b, below_b))):
                    halves = ranked[:].bitcast(U16).rearrange("p (n two) -> p n two", two=2)
                    m = step_done(V.tensor_scalar(mark[:], halves[:, :, 1], high_part[:, j:j + 1], -1.0,
                                                  ALU.subtract, ALU.max))
                    after(m)
                    m = step_done(V.tensor_scalar(mark[:], mark[:], 1.0, 65536.0, ALU.min, ALU.mult))
                    after(m)
                    m = step_done(V.tensor_tensor(ranked[:], mark[:], halves[:, :, 0], ALU.add))
                after(m)

            def decide(r):
                last = {HIGH_BITS: high_part, BITS: limit}
                if r in last:
                    after(step_done(keep_or_not(r - 1, ("decide", (r,), 0), last[r][:])))
                elif r >= 1:
                    keep_or_not(r - 1, ("decide", (r,), 0), tried[:]).then_inc(sem("tried"), 1)
                if r == 0:
                    magnitudes()
                if r == HIGH_BITS:
                    low_keys()
                if r in (0, HIGH_BITS):
                    V.memset(tried[:], bit_of(r) - 0.5).then_inc(sem("tried"), 1)

            def count_below(r):
                if r >= 1:
                    wait_filled(dve, "decide", (r,))
                dve.wait_ge(sem("tried"), r + 1)
                for j, (ranked, mark, cols) in enumerate(((ranked_w, below, BY_DVE), (ranked_b, below_b, RB))):
                    V.tensor_scalar(mark[:, 0:cols], searched(ranked, r)[:, 0:cols], tried[:, j:j + 1], None,
                                    ALU.is_lt, ALU.add, accum_out=counted[:, j:j + 1]).then_inc(sem("counted"), 1)
                less = 0.5 if r + 1 in (HIGH_BITS, BITS) else 0.5 * bit_of(r)
                V.tensor_scalar(base[:], tried[:], -less, None, ALU.add).then_inc(sem("based"), 1)

            def perturb(src, dst, n, j, w, done):
                lo, hi = limits[:, j, 2 * w:2 * w + 1], limits[:, j, 2 * w + 1:2 * w + 2]
                after(step_done(V.tensor_scalar(size[:, 0:n].bitcast(I32), src.bitcast(I32), 0x7FFFFFFF, None,
                                                ALU.bitwise_and)))
                step_done(V.tensor_scalar(tier[:, 0:n], size[:, 0:n], hi, -2.0, ALU.is_ge, ALU.mult))
                after(step_done(V.tensor_scalar(tier2[:, 0:n], size[:, 0:n], lo, None, ALU.is_le)))
                after(step_done(V.scalar_tensor_tensor(out=tier[:, 0:n], in0=tier[:, 0:n], scalar=1.0,
                                                       in1=tier2[:, 0:n], op0=ALU.add, op1=ALU.min)))
                after(step_done(V.scalar_tensor_tensor(out=tier2[:, 0:n], in0=tier[:, 0:n], scalar=GAIN, in1=src,
                                                       op0=ALU.mult, op1=ALU.mult)))
                V.tensor_tensor(dst, tier2[:, 0:n], src, ALU.add).then_inc(sem(done), 1)
                dve.wait_ge(sem(done), 1)

            def join_limits():
                step_done(V.tensor_copy(limit_bits[:, 0], high_part[:]))
                after(step_done(V.tensor_copy(limit_bits[:, 1], limit[:])))
                after(step_done(V.tensor_scalar(limit_bits[:, 0], limit_bits[:, 0], 16, None,
                                                ALU.logical_shift_left)))
                after(step_done(V.tensor_tensor(limit_bits[:, 0], limit_bits[:, 0], limit_bits[:, 1],
                                                ALU.bitwise_or)))
                for j in range(2):
                    V.tensor_scalar(picked[:, j], picks[:], limit_bits[:, 0, j:j + 1].bitcast(F32), None,
                                    ALU.mult).then_inc(sem("picked"), 1)
                key = ("limits", (), 0)
                wait_filled(dve, *key)
                drained(V.tensor_copy(limits[:].rearrange("p a b -> p (a b)"), psum(key)[:, 0:8]))
                wait_drained(dve, *key)

            def pool_gate(g):
                half = half_tiles(g)
                wait_drained(dve, "transpose", ("experts", g))
                own = slice(g * B // 2, (g + 1) * B // 2)
                after(step_done(V.tensor_reduce(pooled_T[:, own],
                                                xn_T[:, g * TC:g * TC + TC].rearrange("p (b s) -> p b s", s=S),
                                                AX, ALU.add)))
                V.tensor_copy(xn[:, half].rearrange("p t (b s) -> p (t b) s", b=2),
                              pooled_T[:, own].unsqueeze(2).broadcast_to([P, B // 2, S])).then_inc(sem("pooled"), 1)

            def gate(g):
                half = half_tiles(g)
                key = ("gate", (g,), 0)
                wait_filled(dve, *key)
                wait_loaded(dve, "rows")
                drained(V.scalar_tensor_tensor(out=logits[:, half],
                                               in0=psum(key)[:, 0:TH * E].rearrange("p (t e) -> p t e", e=E),
                                               scalar=1.0 / S, in1=across(row_gate_b), op0=ALU.mult, op1=ALU.add))
                wait_drained(dve, *key)
                for t in range(g * TH, g * TH + TH):
                    m = step_done(V.max(best[:, t], logits[:, t]))
                after(m)
                V.tensor_tensor(weights[:, half], logits[:, half], wide8(best[:, half, 0:1]), ALU.subtract)\
                 .then_inc(sem("gate_shifted"), 1)
                after(step_done(V.tensor_tensor(kept[:, half], logits[:, half], wide8(best[:, half, 1:2]),
                                                ALU.is_ge)))

            def weigh_gate(g):
                half = half_tiles(g)
                dve.wait_ge(sem("gate_exp"), g + 1)
                after(step_done(V.tensor_tensor(weights[:, half], weights[:, half], kept[:, half], ALU.mult)))
                after(step_done(V.tensor_reduce(total[:, half], weights[:, half], AX, ALU.add)))
                after(step_done(V.reciprocal(total[:, half], total[:, half])))
                V.tensor_tensor(gates[:, half], weights[:, half], wide8(total[:, half].unsqueeze(2)), ALU.mult)\
                 .then_inc(sem("gates_ready"), 1)

            def router(g):
                half = half_tiles(g)
                key = ("router", (g,), 0)
                wait_filled(dve, *key)
                drained(V.tensor_tensor(logits[:, half], psum(key)[:, 0:TH * E].rearrange("p (t e) -> p t e", e=E),
                                        across(row_br), ALU.add))
                wait_drained(dve, *key)
                after(step_done(V.tensor_reduce(total[:, half], logits[:, half], AX, ALU.max)))
                V.tensor_tensor(weights[:, half], logits[:, half], wide8(total[:, half].unsqueeze(2)), ALU.subtract)\
                 .then_inc(sem("router_shifted"), 1)

            def weigh_router(g):
                half = half_tiles(g)
                dve.wait_ge(sem("router_exp"), g + 1)
                after(step_done(V.tensor_reduce(share[:, half, 1], weights[:, half, 1:E], AX, ALU.add)))
                after(step_done(V.tensor_tensor(total[:, half], share[:, half, 1], weights[:, half, 0], ALU.add)))
                after(step_done(V.reciprocal(total[:, half], total[:, half])))
                step_done(V.tensor_tensor(share[:, half, 0], weights[:, half, 0], total[:, half], ALU.mult))
                after(step_done(V.tensor_tensor(share[:, half, 1], share[:, half, 1], total[:, half], ALU.mult)))

            after(constants())
            for step, n in todo:
                key = (step, n, 0)
                if step == "norm_stats":
                    norm_stats_(n)
                elif step == "norm":
                    norm(n)
                elif step == "split_bias":
                    wait_loaded(dve, "expert_b")
                    after(step_done(V.tensor_copy(expert_b_part[:, 0], expert_b[:])))
                    after(step_done(V.tensor_tensor(expert_b_rest, expert_b[:], expert_b_part[:, 0], ALU.subtract)))
                    after(step_done(V.tensor_copy(expert_b_part[:, 1], expert_b_rest)))
                    after(step_done(V.tensor_tensor(expert_b_rest, expert_b_rest, expert_b_part[:, 1],
                                                    ALU.subtract)))
                    V.tensor_copy(expert_b_part[:, 2], expert_b_rest).then_inc(sem("bias_split"), 1)
                elif step == "expand_mask":
                    wait_loaded(dve, "mask")
                    after(step_done(V.copy_predicated(mask_add[:], mask_in[:], work[:, 0, 0:TILES])))
                elif step == "clear_values":
                    ones_beside_values()
                elif step == "values0":
                    before = v0_ring.before[(step, n)]
                    wait_filled(dve, *key)
                    if before is not None:
                        wait_filled(dve, "attend0", (2 * before[1][0] + 1,))
                    dst = v0[:, v0_ring.at[(step, n)], :, :, 0:2 * DK0]
                    src = psum(key)[:].rearrange("p (b c v) -> p b c v", b=4, c=HP)
                    keep = pair_mask[:].rearrange("p w d -> p (w d)").unsqueeze(1).unsqueeze(1)
                    drained(V.tensor_tensor(dst, src, keep.broadcast_to([P, 4, HP, 2 * DK0]), ALU.mult))
                elif step in ("scores0", "scores1"):
                    if step == "scores1":
                        wait_loaded(dve, "fside")
                    scores(int(step[-1]), n)
                elif step == "attend0":
                    attend0(n)
                elif step == "project0":
                    half = half_tiles(n[0])
                    wait_filled(dve, *key)
                    drained(V.tensor_tensor(res[:, half], psum(key)[:].rearrange("p (t d) -> p t d", t=TH),
                                            xn[:, half], ALU.add))
                    wait_drained(dve, *key)
                elif step == "bias_x1":
                    half = half_tiles(n[0])
                    wait_loaded(dve, "rows")
                    wait_filled(dve, "transpose", ("x1", n[0]))
                    after(step_done(V.tensor_tensor(x1[:, half], x1[:, half], across(rows["row_b2"]), ALU.add)))
                elif step == "down0":
                    half = half_tiles(n[0])
                    wait_filled(dve, *key)
                    drained(V.tensor_tensor(res[:, half], psum(key)[:].rearrange("p (t d) -> p t d", t=TH),
                                            x1[:, half], ALU.add))
                    wait_drained(dve, *key)
                elif step == "pool_gate":
                    pool_gate(n[0])
                elif step == "gate":
                    gate(n[0])
                elif step == "weigh_gate":
                    weigh_gate(n[0])
                elif step == "add_experts":
                    t = n[0]
                    dve.wait_ge(sem("experts_weighed"), t + 1)
                    V.tensor_reduce(expert_sum[:], work_of("experts", t).rearrange("p h k -> p (h k)")
                                    .rearrange("p (e d) -> p d e", e=E), AX, ALU.add).then_inc(sem("experts_summed"), 1)
                    dve.wait_ge(sem("experts_summed"), t + 1)
                    after(step_done(V.tensor_tensor(xt[:, t], expert_sum[:], xt[:, t], ALU.add)))
                elif step == "sums1":
                    t = n[0]
                    dve.wait_ge(sem("exp1"), t + 1)
                    after(step_done(V.tensor_reduce(row_sum[:, t], work_of("scores1", t), AX, ALU.add)))
                    V.reciprocal(row_inv[:, t], row_sum[:, t]).then_inc(sem("inverse1"), 1)
                elif step == "attend1":
                    t = n[0]
                    wait_filled(dve, *key)
                    drained(V.tensor_tensor(xt[:, t], psum(key)[:, 0:D], xt[:, t], ALU.add))
                    wait_drained(dve, *key)
                elif step == "decide":
                    decide(n[0])
                elif step == "count":
                    count_below(n[0])
                elif step == "combine":
                    r = n[0]
                    dve.wait_ge(sem("counted"), 2 * (r + 1))
                    dve.wait_ge(sem("signs_ready"), r + 1)
                    V.scalar_tensor_tensor(out=counted[:, 0:1], in0=signs[:], scalar=0.5, in1=counted[:, 0:1],
                                           op0=ALU.mult, op1=ALU.add).then_inc(sem("combined"), 1)
                elif step == "limits":
                    join_limits()
                elif step == "perturb":
                    wait_loaded(dve, "ffn1")
                    flat = lambda w: w.rearrange("p c d -> p (c d)")
                    perturb(*{"b1": (b1_1, b1_p[:], FC, 1, 0), "w1": (w1_1[:], w1_p, F, 0, 0),
                              "w2": (flat(w2_1[:]), flat(w2_p), F, 0, 1),
                              "b2": (rows["row_y0"][:], rows["row_y1"][:], D, 1, 1)}[n[0]], f"{n[0]}_perturbed")
                elif step == "router":
                    router(n[0])
                elif step == "weigh_router":
                    weigh_router(n[0])
                elif step == "down1":
                    g, e = n
                    half = half_tiles(g)
                    wait_loaded(dve, "rows")
                    wait_filled(dve, *key)
                    drained(V.tensor_tensor(res[:, half], psum(key)[:].rearrange("p (t d) -> p t d", t=TH),
                                            across(rows[f"row_y{e}"]), ALU.add))
                    wait_drained(dve, *key)
                    for t in range(g * TH, g * TH + TH):
                        ins = V.scalar_tensor_tensor(out=xt[:, t], in0=res[:, t], scalar=share[:, t, e:e + 1],
                                                     in1=xt[:, t], op0=ALU.mult, op1=ALU.add)
                        if e == 0:
                            m = step_done(ins)
                        else:
                            ins.then_inc(sem("x_done"), 1)
                    if e == 0:
                        after(m)

        @block.tensor
        def _(pe):
            def begin(key):
                if rings.before[key] is not None:
                    wait_drained(pe, *rings.before[key])
                return psum(key)

            def end(key, ins):
                ins.then_inc(sem(f"{rings.slot[key][0]}_filled"), 1)

            def flat(ps):
                return ps[:].rearrange("p a n -> p (a n)")

            def transposes(key, sources):
                ps = begin(key)
                dst = flat(ps) if rings.slot[key][0] == "big" else ps[:]
                for j, src in enumerate(sources):
                    rows_in = src.shape[0]
                    ins = nc.tensor.transpose(dst[:, j * P:j * P + rows_in], src, ident[0:rows_in, 0:rows_in])
                end(key, ins)

            def count(r, key):
                ps = begin(key)
                pe.wait_ge(sem("combined"), r + 1)
                end(key, nc.tensor.matmul(ps[:, 0:2], groups[:], counted[:], start=True, stop=True))

            pe.wait_ge(sem("ident_ready"), 1)
            pe.wait_ge(sem("ones_ready"), 1)
            for step, n in todo:
                key = (step, n, 0)
                if step == "transpose_w0":
                    wait_loaded(pe, "w0")
                    transposes(key, [wq0[:], wo0[:], gate_w[:], b1_rows[:]])
                elif step == "transpose_ctx":
                    wait_loaded(pe, "ctx")
                    transposes(key, [ctx_tok[:, t] for t in range(TILES)])
                elif step == "transpose":
                    wait_norm(pe, *n)
                    src = x1 if n[0] in ("x1", "router") else xn
                    transposes(key, [src[:, t] for t in range(n[1] * TH, n[1] * TH + TH)])
                elif step == "project_k0":
                    ps = begin(key)
                    wait_drained(pe, "transpose_w0")
                    wait_drained(pe, "transpose_ctx")
                    for g in range(HALVES):
                        ins = nc.tensor.matmul(ps[:, g], wq0_T[:], ctx_T[:, g * TC:g * TC + TC], start=True, stop=True)
                    end(key, ins)
                elif step == "project_q0":
                    g = n[0]
                    ps = begin(key)
                    wait_drained(pe, "transpose", ("attn0", g))
                    wait_drained(pe, "transpose_w0")
                    end(key, nc.tensor.matmul(ps[:], wq0_T[:], xn_T[:, g * TC:g * TC + TC], start=True, stop=True))
                elif step == "weight_T":
                    if n[0] == "ffn0":
                        wait_loaded(pe, "ffn0_w")
                        transposes(key, [w1_0[:, c] for c in range(FC)]
                                   + [w2_0[:, c * P:c * P + P] for c in range(FC)])
                    elif n[0] == "experts":
                        wait_loaded(pe, "expert_w")
                        transposes(key, [expert_w[:, e] for e in range(E)])
                    else:
                        wait_loaded(pe, "w1_qk")
                        transposes(key, [wo1[:, h] for h in range(HP)])
                elif step == "fold_weights":
                    ps = begin(key)
                    wait_loaded(pe, "w1_qk")
                    if n[0] == "vo":
                        wait_loaded(pe, "w1_v")
                        wait_drained(pe, "weight_T", ("wo1",))
                    left, right = (wk1, wq1) if n[0] == "qk" else (wv1, wo1_T)
                    for j in range(HP):
                        h = n[1] * HP + j
                        rows_h = slice(DK1 * (h % 2), DK1 * (h % 2) + DK1)
                        ins = nc.tensor.matmul(ps[:, j % 2, (j // 2) * D:(j // 2) * D + D], left[rows_h, h // 2],
                                               right[rows_h, h // 2], start=True, stop=True)
                    end(key, ins)
                elif step == "values0":
                    ps = begin(key)
                    wait_drained(pe, "transpose_w0")
                    wait_drained(pe, "transpose_ctx")
                    for b in range(4):
                        at = (4 * n[0] + b) * KEYS
                        for h2 in range(2):
                            ins = nc.tensor.matmul(ps[KEYS * h2:KEYS * h2 + KEYS, b * D:b * D + D],
                                                   ctx_T[:, at:at + KEYS], wq0_T[:], start=True, stop=True)
                    end(key, ins)
                elif step in ("scores0", "scores1"):
                    t = n[0]
                    ps = begin(key)
                    if step == "scores0":
                        wait_drained(pe, "project_q0", (t // TH,))
                        pe.wait_ge(sem("keys0_expanded"), t + 1)
                        queries, first = q0_T, 0
                        by_head = wide[:, wide_ring.at[("expand_keys0", n)]].rearrange("p (h k) -> p h k", h=H)
                    else:
                        wait_drained(pe, "transpose", ("attn1", t // TH))
                        wait_drained(pe, "keys1", (H - 1,))
                        queries, first = xn_T, t * P
                        by_head = keys1
                    for a2 in range(2):
                        for b in range(2):
                            at = (2 * t + b) * KEYS
                            ins = nc.tensor.matmul(ps[S * b:S * b + S, a2], queries[:, at:at + S],
                                                   by_head[:, a2 * HP:a2 * HP + HP,
                                                           first + b * KEYS:first + b * KEYS + KEYS],
                                                   start=True, stop=True)
                    end(key, ins)
                elif step in ("transpose_probs0", "transpose_probs1"):
                    t = n[0]
                    pe.wait_ge(sem("exp0" if step == "transpose_probs0" else "probs1"), t + 1)
                    probs = work_of("scores" + step[-1], t)
                    transposes(key, [probs[:, 2 * h:2 * h + 2].rearrange("p h k -> p (h k)") for h in range(HP)])
                elif step == "attend0":
                    t = n[0]
                    ps = begin(key)
                    wait_drained(pe, "transpose_probs0", n)
                    wait_drained(pe, "values0", (t // 2,))
                    values = v0[:, v0_ring.at[("values0", (t // 2,))], 2 * (t % 2):2 * (t % 2) + 2]
                    for h in range(HP):
                        ins = nc.tensor.matmul(ps[:, h * 2 * VW:(h + 1) * 2 * VW], probs_of(0, t)[:, h],
                                               values[:, :, h], start=True, stop=True)
                    end(key, ins)
                elif step == "transpose_att":
                    wait_drained(pe, "attend0", (n[0] * TH + TH - 1,))
                    transposes(key, [att[:, j] for j in range(TH)])
                elif step == "project0":
                    ps = begin(key)
                    wait_drained(pe, "transpose_att", n)
                    for j in range(TH):
                        ins = nc.tensor.matmul(ps[:, j * D:j * D + D], att_T[:, j * P:j * P + P], wo0_T[:],
                                               start=True, stop=True)
                    end(key, ins)
                elif step == "up0":
                    g, f = n
                    ps = begin(key)
                    wait_drained(pe, "transpose", ("x1", g))
                    wait_drained(pe, "weight_T", ("ffn0",))
                    for j in range(2):
                        ins = nc.tensor.matmul(ps[:, j], w1_0T[:, (f + j) * P:(f + j + 1) * P],
                                               xn_T[:, g * TC:g * TC + TC], start=True, stop=True)
                    end(key, ins)
                elif step in ("down0", "down1"):
                    ps = begin(key)
                    if step == "down0":
                        wait_drained(pe, "up0", (n[0], FC - 2))
                        wait_drained(pe, "weight_T", ("ffn0",))
                        layer, w = hidden[:, n[0]], w2_0T
                    else:
                        wait_loaded(pe, "ffn1")
                        wait_drained(pe, "up1", (*n, FC - 2))
                        if n[1] == 1:
                            pe.wait_ge(sem("w2_perturbed"), 1)
                        layer, w = hidden[:, n[1]], (w2_1, w2_p)[n[1]]
                    for j in range(TH):
                        for f in range(FC):
                            ins = nc.tensor.matmul(ps[:, j * D:j * D + D], layer[:, f, j * P:j * P + P],
                                                   w[:, f], start=(f == 0), stop=(f == FC - 1))
                    end(key, ins)
                elif step == "keys1":
                    ps = begin(key)
                    wait_drained(pe, "transpose_ctx")
                    wait_drained(pe, "fold_weights", ("qk", n[0] // HP))
                    for g in range(HALVES):
                        ins = nc.tensor.matmul(ps[:, g], qk_w[:, n[0]], ctx_T[:, g * TC:g * TC + TC],
                                               start=True, stop=True)
                    end(key, ins)
                elif step == "gate":
                    ps = begin(key)
                    pe.wait_ge(sem("pooled"), n[0] + 1)
                    for j in range(TH):
                        ins = nc.tensor.matmul(ps[:, j * E:j * E + E], xn[:, n[0] * TH + j], gate_w_T[:],
                                               start=True, stop=True)
                    end(key, ins)
                elif step == "experts":
                    t = n[0]
                    ps = begin(key)
                    pe.wait_ge(sem("bias_rows"), 48)
                    wait_drained(pe, "transpose", ("experts", t // TH))
                    wait_drained(pe, "weight_T", ("experts",))
                    for j in range(2):
                        nc.tensor.matmul(ps[:, j], ones_bf[:], expert_b_rows[:, j * 512:j * 512 + 512],
                                         start=True, stop=False)
                        ins = nc.tensor.matmul(ps[:, j], xn_T[:, t * P:t * P + P],
                                               expert_w_T[:, 4 * j:4 * j + 4].rearrange("p e d -> p (e d)"),
                                               start=False, stop=True)
                    end(key, ins)
                elif step == "values1":
                    t = n[0]
                    wait_drained(pe, "transpose_ctx")
                    wait_drained(pe, "fold_weights", ("vo", 1))
                    for b in range(2):
                        key = (step, n, b)
                        ps = begin(key)
                        at = (2 * t + b) * KEYS
                        for j in range(2):
                            for h2 in range(2):
                                heads_j = vo_w[:].rearrange("p (h w) d -> p w h d", w=2)[:, h2, 4 * j:4 * j + 4]
                                ins = nc.tensor.matmul(ps[KEYS * h2:KEYS * h2 + KEYS, j], ctx_T[:, at:at + KEYS],
                                                       heads_j, start=True, stop=True)
                        end(key, ins)
                elif step == "attend1":
                    t = n[0]
                    ps = begin(key)
                    wait_drained(pe, "transpose_probs1", n)
                    wait_drained(pe, "values1", n, 1)
                    values = wide[:, wide_ring.at[("values1", n)]].rearrange("p (b h d) -> p b h d", b=2, h=HP)
                    for h in range(HP):
                        for b in range(2):
                            ins = nc.tensor.matmul(ps[S * b:S * b + S, 0:D], probs_of(1, t)[:, h, S * b:S * b + S],
                                                   values[:, b, h], start=(h == 0), stop=(h == HP - 1))
                    end(key, ins)
                elif step == "router":
                    ps = begin(key)
                    wait_drained(pe, "transpose", ("router", n[0]))
                    wait_loaded(pe, "ffn1")
                    for j in range(TH):
                        at = (n[0] * TH + j) * P
                        ins = nc.tensor.matmul(ps[:, j * E:j * E + E], ctx_T[:, at:at + P], wr[:],
                                               start=True, stop=True)
                    end(key, ins)
                elif step == "decide" and n[0] >= 1:
                    count(n[0] - 1, key)
                elif step == "limits":
                    ps = begin(key)
                    pe.wait_ge(sem("picked"), 2)
                    end(key, nc.tensor.matmul(ps[:, 0:8], ones[:], picked[:].rearrange("p a b -> p (a b)"),
                                              start=True, stop=True))
                elif step == "up1":
                    g, e, f = n
                    ps = begin(key)
                    wait_drained(pe, "transpose", ("moe", g))
                    wait_loaded(pe, "ffn1")
                    if e == 1:
                        pe.wait_ge(sem("w1_perturbed"), 1)
                    w = (w1_1[:], w1_p)[e]
                    for j in range(2):
                        ins = nc.tensor.matmul(ps[:, j], w[:, (f + j) * P:(f + j + 1) * P],
                                               xn_T[:, g * TC:g * TC + TC], start=True, stop=True)
                    end(key, ins)


_INS = ['x', 'ctx_1024', 'fside_Bx1xSxS2_0', 'mask_Bx1xSxS2_bf0', 'L0_xattn_Wq', 'L0_xattn_Wo', 'L0_xattn_W1',
        'L0_xattn_b1', 'L0_xattn_W2', 'L0_xattn_b2', 'L0_xattn_g1', 'L0_xattn_be1', 'L0_xattn_g2', 'L0_xattn_be2',
        'L0_ffn_gate_w', 'L0_ffn_gate_b', 'L0_ffn_expert_w', 'L0_ffn_expert_b', 'L1_xattn_Wq', 'L1_xattn_Wk',
        'L1_xattn_Wv', 'L1_xattn_Wo', 'L1_ffn_W1', 'L1_ffn_b1', 'L1_ffn_W2', 'L1_ffn_b2', 'L1_ffn_ln_gamma',
        'L1_ffn_ln_beta', 'L1_ffn_Wr', 'L1_ffn_br']


def kernel(**inputs):
    import numpy as _np
    import concourse.bacc as _bacc
    from concourse import mybir as _mybir
    from concourse.bass_utils import run_bass_kernel_spmd as _run

    nc = _bacc.Bacc("TRN2", target_bir_lowering=False, num_devices=1)
    arrays, args = {}, {}
    for name in _INS:
        a = _np.ascontiguousarray(inputs[name])
        arrays[f"in_{name}_dram"] = a
        args[name] = nc.dram_tensor(f"in_{name}_dram", a.shape, _mybir.dt.from_np(a.dtype), kind="ExternalInput").ap()
    shape = inputs["x"].shape
    out = nc.dram_tensor("out_0_dram", shape, _mybir.dt.float32, kind="ExternalOutput").ap()
    build(nc, args, out)
    r = _run(nc, [arrays], core_ids=[0])
    return r.results[0]["out_0_dram"]
```
